# Optimizing a Trainium2 kernel written in Bass

```python
import numpy as np
import jax
import jax.numpy as jnp

def _softmax(x, axis=-1):
    return jax.nn.softmax(x, axis=axis)

def _gelu(x):
    return jax.nn.gelu(x, approximate=True)

def _silu(x):
    return jax.nn.silu(x)

def _sigmoid(x):
    return jax.nn.sigmoid(x)

def _layernorm(x, axis=-1, eps=1e-05):
    m = jnp.mean(x, axis=axis, keepdims=True)
    v = jnp.var(x, axis=axis, keepdims=True)
    return (x - m) / jnp.sqrt(v + eps)

def _scatter_add(tgt, idx, src, axis=0):
    return tgt.at[idx].add(src)

def _segment_sum(src, seg, n):
    return jax.ops.segment_sum(src, seg, n)
kernel_name = 'mk_adaln_ffn_d1_seqx_r2_6b2e8a'

def setup_inputs(seed: int=0):
    np.random.seed(seed)
    _w = jnp.asarray

    def _rec_inputs():
        import jax
        import jax.numpy as jnp
        _rk = jax.random.key(seed)
        x = -0.000125 + 0.9999 * jax.random.normal(jax.random.fold_in(_rk, 1), (32, 128, 2048), jnp.float32)
        _lenS = 128 - jax.random.randint(jax.random.fold_in(_rk, 7), (32,), 0, max(1, 128 // 4) + 1, jnp.int32)
        _lenS2 = 128 - jax.random.randint(jax.random.fold_in(_rk, 8), (32,), 0, max(1, 128 // 4) + 1, jnp.int32)
        cond_128 = 0.0061147 + 1.02565 * jax.random.normal(jax.random.fold_in(_rk, 11), (32, 128), jnp.float32)
        return (x, cond_128)
    x, cond_128 = _rec_inputs()

    def _L0_cond_setup():
        import jax, jax.numpy as jnp
        import numpy as np
        K = 8
        T = 1.0
        D_EMBD = 128
        IN_C = 128
        OUT_C = 128
        BS = 32
        H = 2048
        HID = 128
        key = jax.random.key(seed)
        ks = jax.random.split(key, 10)
        s = lambda fan_in: 1.0 / np.sqrt(fan_in)
        return {'x': jax.random.normal(ks[0], (BS, IN_C, H), dtype=jnp.float32), 'embedding': jax.random.normal(ks[1], (BS, D_EMBD), dtype=jnp.float32), 'W0': jax.random.normal(ks[2], (D_EMBD, HID), dtype=jnp.float32) * s(D_EMBD), 'b0': jnp.zeros((HID,), dtype=jnp.float32), 'W1': jax.random.normal(ks[3], (HID, HID), dtype=jnp.float32) * s(HID), 'b1': jnp.zeros((HID,), dtype=jnp.float32), 'W2': jax.random.normal(ks[4], (HID, K), dtype=jnp.float32) * s(HID), 'b2': jnp.zeros((K,), dtype=jnp.float32), 'weight': jax.random.normal(ks[5], (K, OUT_C, IN_C, 1), dtype=jnp.float32) * s(IN_C), 'bias_k': jax.random.normal(ks[6], (K, OUT_C), dtype=jnp.float32) * 0.1}
    _L0_cond_all = _L0_cond_setup()
    _L0_cond_in = {k: v for k, v in _L0_cond_all.items() if k in ('W0', 'b0', 'W1', 'b1', 'W2', 'b2', 'weight', 'bias_k')}
    del _L0_cond_all

    def _L0_ffn_setup():
        import jax, jax.numpy as jnp
        import numpy as np

        @jax.custom_vjp
        def ste_sign(w):
            return jnp.sign(w)

        def _ste_fwd(w):
            return (jnp.sign(w), w)

        def _ste_bwd(w, g):
            mask = ((w > -1) & (w < 1)).astype(g.dtype)
            return (g * mask,)
        ste_sign.defvjp(_ste_fwd, _ste_bwd)
        key = jax.random.key(seed)
        k = jax.random.split(key, 6)
        B, S, H, O, E = (4, 1024, 2048, 2048, 8)
        return {'x': jax.random.normal(k[0], (B, S, H), dtype=jnp.float32), 'weight': jax.random.normal(k[1], (O, H), dtype=jnp.float32) * 0.02, 'bias': jax.random.normal(k[2], (O,), dtype=jnp.float32) * 0.02, 'gate_w': jax.random.normal(k[3], (E, H), dtype=jnp.float32) * 0.02, 'in_channel_scale': jax.random.normal(k[4], (E, H), dtype=jnp.float32), 'out_channel_scale': jax.random.normal(k[5], (E, O), dtype=jnp.float32)}
    _L0_ffn_all = _L0_ffn_setup()
    _L0_ffn_in = {k: v for k, v in _L0_ffn_all.items() if k in ('weight', 'bias', 'gate_w', 'in_channel_scale', 'out_channel_scale')}
    del _L0_ffn_all
    return {'x': x, 'cond_128': cond_128, 'L0_cond_W0': _L0_cond_in['W0'], 'L0_cond_b0': _L0_cond_in['b0'], 'L0_cond_W1': _L0_cond_in['W1'], 'L0_cond_b1': _L0_cond_in['b1'], 'L0_cond_W2': _L0_cond_in['W2'], 'L0_cond_b2': _L0_cond_in['b2'], 'L0_cond_weight': _L0_cond_in['weight'], 'L0_cond_bias_k': _L0_cond_in['bias_k'], 'L0_ffn_weight': _L0_ffn_in['weight'], 'L0_ffn_bias': _L0_ffn_in['bias'], 'L0_ffn_gate_w': _L0_ffn_in['gate_w'], 'L0_ffn_in_channel_scale': _L0_ffn_in['in_channel_scale'], 'L0_ffn_out_channel_scale': _L0_ffn_in['out_channel_scale']}

def reference(x, cond_128, L0_cond_W0, L0_cond_b0, L0_cond_W1, L0_cond_b1, L0_cond_W2, L0_cond_b2, L0_cond_weight, L0_cond_bias_k, L0_ffn_weight, L0_ffn_bias, L0_ffn_gate_w, L0_ffn_in_channel_scale, L0_ffn_out_channel_scale):
    import jax
    import jax.numpy as jnp

    def _L0_cond_ref(x, embedding, W0, b0, W1, b1, W2, b2, weight, bias_k):
        import jax, jax.numpy as jnp
        import numpy as np
        K = 8
        T = 1.0
        D_EMBD = 128
        IN_C = 128
        OUT_C = 128
        BS = 32
        H = 2048
        HID = 128
        h = jax.nn.gelu(embedding @ W0 + b0, approximate=False)
        h = jax.nn.gelu(h @ W1 + b1, approximate=False)
        att = jax.nn.softmax((h @ W2 + b2) / T, axis=-1)
        agg_w = jnp.einsum('bk,koi->boi', att, weight[..., 0])
        agg_b = att @ bias_k
        out = jnp.einsum('boi,bih->boh', agg_w, x) + agg_b[:, :, None]
        return out

    def _L0_ffn_ref(x, weight, bias, gate_w, in_channel_scale, out_channel_scale):
        import jax, jax.numpy as jnp
        import numpy as np

        @jax.custom_vjp
        def ste_sign(w):
            return jnp.sign(w)

        def _ste_fwd(w):
            return (jnp.sign(w), w)

        def _ste_bwd(w, g):
            mask = ((w > -1) & (w < 1)).astype(g.dtype)
            return (g * mask,)
        ste_sign.defvjp(_ste_fwd, _ste_bwd)
        B, S, H = x.shape
        xf = x.reshape(-1, H)
        router_logits = xf @ gate_w.T
        routing = jax.nn.softmax(router_logits.astype(jnp.float32), axis=1).astype(x.dtype)
        in_scale = routing @ in_channel_scale
        out_scale = routing @ out_channel_scale
        wb = ste_sign(weight)
        out = xf * in_scale @ wb.T * out_scale + bias
        return out.reshape(B, S, -1)
    x = x + _L0_ffn_ref(_L0_cond_ref(x, cond_128, L0_cond_W0, L0_cond_b0, L0_cond_W1, L0_cond_b1, L0_cond_W2, L0_cond_b2, L0_cond_weight, L0_cond_bias_k), L0_ffn_weight, L0_ffn_bias, L0_ffn_gate_w, L0_ffn_in_channel_scale, L0_ffn_out_channel_scale)
    return x

_drawn_inputs = setup_inputs


def setup_inputs(seed=0):
    import zlib

    import numpy as np

    out = dict(_drawn_inputs(seed))
    spreads = {'L0_cond_b0': (0.0, 0.1), 'L0_cond_b1': (0.0, 0.1), 'L0_cond_b2': (0.0, 0.1)}
    factors = {'L0_ffn_bias': 6.988}
    for name, (base, spread) in spreads.items():
        noise = np.random.default_rng([zlib.crc32(name.encode()), seed]).standard_normal(out[name].shape)
        drawn = base * np.exp(spread * noise) if base else spread * noise
        out[name] = jnp.asarray(drawn.astype(out[name].dtype))
    for name, factor in factors.items():
        out[name] = (out[name] * factor).astype(out[name].dtype)
    return out
```

```python
from contextlib import ExitStack

import concourse.bass as bass
from concourse import mybir

ALU = mybir.AluOpType
ACT = mybir.ActivationFunctionType
AX_X = mybir.AxisListType.X
F32 = mybir.dt.float32
F32R = mybir.dt.float32r
BF16 = mybir.dt.bfloat16

P = 128
NW = 512
PARTS = 3
STAGES = 3
DMA = 16


def adaln_ffn(nc, x, embT, W0, b0, W1, b1, W2, b2, mixT, mix_bias, ffn_wT, ffn_bias, gateT, scales, out):
    B, T, H = x.shape
    E = W2.shape[1]
    NC = H // P
    NB = ffn_wT.shape[1] // NW
    GC = NW // P
    NG = NC // GC
    R = PARTS * PARTS * E
    UNITS = NB * NC
    HH = P // E
    MM = 2 * NC
    assert T == P and NG == NB and B % 2 == 0

    BIAS_AT = 8
    Y_AT = 16
    GATE_AT = 38
    ROUTE_AT = 92
    SCALE_AT = 96

    with ExitStack() as ctx:
        def sb(name, shape, dt=F32):
            return ctx.enter_context(nc.sbuf_tensor(name, shape, dt))

        def bank(name):
            return ctx.enter_context(nc.psum_tensor(name, [P, NW], F32))

        def sem(name):
            return ctx.enter_context(nc.semaphore(name))

        signs = sb("signs", [P, NC, NB * NW], F32R)
        stage = sb("stage", [P, STAGES, NW])
        xs = [sb(f"xs{i}", [P, H]) for i in range(2)]
        y = sb("y", [P, NC, T])
        hi = [sb(f"hi{i}", [P, NC, T], F32R) for i in range(2)]
        lo = [sb(f"lo{i}", [P, NC, T], F32R) for i in range(2)]
        results = [sb(f"results{i}", [P, NW]) for i in range(2)]
        out_scale = sb("out_scale", [P, NW])
        bias_rows = sb("bias_rows", [P, NB * NW])
        in_stack = sb("in_stack", [R, H], BF16)
        out_stack = sb("out_stack", [R, NB * NW], BF16)
        mix_w = sb("mix_w", [P, E, P])
        mix_b = sb("mix_b", [E, P])
        mixed = sb("mixed", [P, P])
        mixed_b = sb("mixed_b", [E, P])
        bias_y = sb("bias_y", [P, T])
        gate = sb("gate", [P, NC, 2 * E], F32R)
        att_rows = sb("att_rows", [P, B, E])
        att_q = sb("att_q", [P, E])
        attT = sb("attT", [E, B])
        logits = sb("logits", [P, E])
        top = sb("top", [P, 1])
        exps = sb("exps", [P, E])
        total = sb("total", [P, 1])
        inverse = sb("inverse", [P, 1])
        route = sb("route", [P, E])
        rest = sb("rest", [P, 2, E])
        parts = sb("parts", [P, PARTS, PARTS, E], BF16)
        routeT = [sb(f"routeT{i}", [R, T], BF16) for i in range(2)]
        ones = sb("ones", [32, P])
        unit32 = sb("unit32", [32, 32])
        unit = sb("unit", [P, P], BF16)
        emb = sb("emb", [P, B])
        w0 = results[0][:, 0:P]
        w1 = results[0][:, P:2 * P]
        att_wide = results[0][0:B, 2 * P:2 * P + B * E].rearrange("b (c e) -> b c e", e=E)
        cut_in = results[1][:, 0:2 * P].rearrange("p (s f) -> p s f", s=2)
        cut_rest = results[1][:, 2 * P:4 * P].rearrange("p (s f) -> p s f", s=2)
        gate_in = out_scale[:, PARTS * P:4 * P].rearrange("p (c e) -> p c e", e=E)
        cuts = out_scale[:, 0:PARTS * P].bitcast(BF16).rearrange("p (j s f) -> p j s f", j=PARTS, s=2)
        w2 = sb("w2", [P, E])
        b0c = sb("b0c", [P, 1])
        b1c = sb("b1c", [P, 1])
        b2r = sb("b2r", [B, E])
        h1 = sb("h1", [P, B])
        h2 = sb("h2", [P, B])
        att = sb("att", [B, E])

        main = [bank(f"main{i}") for i in range(2)]
        ring = [bank(f"ring{g}") for g in range(NG)]
        scale_bank = bank("scale_bank")
        small = bank("small")
        gate_sum = small[:, 0:2 * E]
        bias_sum = small[:, P:2 * P]
        routeT_ps = small[0:R, 2 * P:2 * P + T // 2].bitcast(BF16)

        smalls_in = sem("smalls_in")
        mixes_in = sem("mixes_in")
        gates_in = sem("gates_in")
        bias_in = sem("bias_in")
        x_in = [sem(f"x_in{i}") for i in range(2)]
        w_in = [sem(f"w_in{i}") for i in range(STAGES)]
        w_signed = sem("w_signed")
        constants = sem("constants")
        cut_steps = sem("cut_steps")
        stacked = sem("stacked")
        gate_cut = sem("gate_cut")
        hidden = sem("hidden")
        gelu_done = sem("gelu_done")
        att_steps = sem("att_steps")
        att_exp = sem("att_exp")
        att_spread = sem("att_spread")
        att_kept = sem("att_kept")
        mix_steps = sem("mix_steps")
        mixed_ready = sem("mixed_ready")
        bias_mm = sem("bias_mm")
        bias_y_ready = sem("bias_y_ready")
        y_mm = sem("y_mm")
        y_ready = sem("y_ready")
        y_hi = sem("y_hi")
        y_lo = sem("y_lo")
        gates_mm = sem("gates_mm")
        route_steps = sem("route_steps")
        route_exp = sem("route_exp")
        parts_ready = sem("parts_ready")
        route_mm = sem("route_mm")
        route_ready = sem("route_ready")
        scale_mm = sem("scale_mm")
        z_ready = sem("z_ready")
        z_hi = sem("z_hi")
        z_lo = sem("z_lo")
        out_scale_mm = sem("out_scale_mm")
        out_scale_ready = sem("out_scale_ready")
        main_mm = sem("main_mm")
        scaled = sem("scaled")
        result_ready = sem("result_ready")
        x_biased = sem("x_biased")
        stored = [sem(f"stored{i}") for i in range(2)]

        block = ctx.enter_context(nc.Block())

        def chunk(c):
            return slice(c * P, (c + 1) * P)

        def columns(n):
            return slice(n * NW, (n + 1) * NW)

        def group(g):
            return slice(g * GC, (g + 1) * GC)

        def by_chunk(b):
            return b[:, :].rearrange("p (c t) -> p c t", c=GC)

        def steps(engine, step):
            for b in range(2):
                step(b, 0, b, True, True)
            with engine.Fori(1, B // 2 - 1) as pair:
                for odd in range(2):
                    step(2 * pair + odd, pair, odd, True, False)
            for b in (B - 2, B - 1):
                step(b, B // 2 - 1, b % 2, b + 1 < B, False)

        SMALLS = 7
        w_units = ffn_wT.rearrange("(c p) (n w) -> n c p w", p=P, w=NW)

        @block.sync
        def _(sp):
            for dst, src in ((emb[:, :], embT), (w0, W0), (b0c[:, :], b0), (w1, W1), (b1c[:, :], b1), (w2[:, :], W2)):
                sp.dma_start(dst, src).then_inc(smalls_in, DMA)
            sp.dma_start(b2r[:, :], b2).then_inc(smalls_in, DMA)
            sp.dma_start(mix_w[:, :, :], mixT).then_inc(mixes_in, DMA)
            sp.dma_start(mix_b[:, :], mix_bias).then_inc(mixes_in, DMA)
            for n in range(NB):
                sp.dma_start(xs[0][:, columns(n)], x[0, :, columns(n)]).then_inc(x_in[0], DMA)
            sp.dma_start(gate_in[:, :, :], gateT).then_inc(gates_in, DMA)
            sp.dma_start(cut_in[:, :, :], scales).then_inc(gates_in, DMA)
            for n in range(NB):
                sp.dma_start(xs[1][:, columns(n)], x[1, :, columns(n)]).then_inc(x_in[1], DMA)
            sp.dma_start(bias_rows[:, :], ffn_bias.partition_broadcast(P)).then_inc(bias_in, DMA)
            sp.wait_ge(cut_steps, 5)
            for i in range(PARTS):
                for j in range(PARTS):
                    for s, stack in enumerate((in_stack, out_stack)):
                        row = (PARTS * i + j) * E
                        sp.dma_start(stack[row:row + E, :].rearrange("e (h f) -> e h f", f=P),
                                     cuts[:, j, s, :]).then_inc(stacked, DMA)

            def step(b, pair, odd, more, early):
                for n in range(NB):
                    sp.wait_ge(result_ready, NB * b + n + 1)
                    sp.dma_start(out[bass.ds(b, 1), :, columns(n)].rearrange("o p w -> (o p) w"),
                                 results[n % 2][:, :]).then_inc(stored[n % 2], DMA)
                    if isinstance(b, int) and b + 2 >= B:
                        continue
                    sp.dma_start(xs[odd][:, columns(n)],
                                 x[bass.ds(b + 2, 1), :, columns(n)].rearrange("o p w -> (o p) w"))\
                      .then_inc(x_in[odd], DMA)

            steps(sp, step)
            for i in range(2):
                sp.wait_ge(stored[i], DMA * B * NB // 2)

        @block.gpsimd
        def _(pool):
            nc.gpsimd.memset(unit32[:, :], 0.0).then_inc(constants, 1)
            nc.gpsimd.memset(unit[:, :], 0.0).then_inc(constants, 1)
            nc.gpsimd.memset(ones[:, :], 1.0).then_inc(constants, 1)
            pool.wait_ge(constants, 3)
            for m, n in ((unit32, 32), (unit, P)):
                nc.gpsimd.affine_select(out=m[:, :], in_=m[:, :], compare_op=ALU.not_equal, fill=1.0,
                                        base=0, pattern=[[-1, n]], channel_multiplier=1).then_inc(constants, 1)
            pool.wait_ge(gates_in, 2 * DMA)
            nc.gpsimd.tensor_copy(gate[:, :, 0:E], gate_in[:, :, :]).then_inc(gate_cut, 1)
            nc.gpsimd.tensor_copy(cuts[:, 0, :, :], cut_in[:, :, :]).then_inc(cut_steps, 1)
            pool.wait_ge(gate_cut, 1)
            nc.gpsimd.tensor_tensor(gate[:, :, E:2 * E], gate_in[:, :, :], gate[:, :, 0:E].bitcast(F32),
                                    ALU.subtract).then_inc(gate_cut, 1)
            pool.wait_ge(cut_steps, 1)
            nc.gpsimd.tensor_tensor(cut_rest[:, :, :], cut_in[:, :, :], cuts[:, 0, :, :],
                                    ALU.subtract).then_inc(cut_steps, 1)
            pool.wait_ge(cut_steps, 2)
            nc.gpsimd.tensor_copy(cuts[:, 1, :, :], cut_rest[:, :, :]).then_inc(cut_steps, 1)
            pool.wait_ge(cut_steps, 3)
            nc.gpsimd.tensor_tensor(cut_rest[:, :, :], cut_rest[:, :, :], cuts[:, 1, :, :],
                                    ALU.subtract).then_inc(cut_steps, 1)
            pool.wait_ge(cut_steps, 4)
            nc.gpsimd.tensor_copy(cuts[:, 2, :, :], cut_rest[:, :, :]).then_inc(cut_steps, 1)

            def add_bias(q, odd):
                pool.wait_ge(y_mm, NG * q + NG)
                for n in range(NB):
                    nc.gpsimd.tensor_tensor(xs[odd][:, columns(n)], xs[odd][:, columns(n)],
                                            bias_rows[:, columns(n)], ALU.add).then_inc(x_biased, 1)

            pool.wait_ge(bias_in, DMA)
            add_bias(0, 0)

            def step(b, pair, odd, more, early):
                if more:
                    add_bias(b + 1, 1 - odd)

            steps(pool, step)

        @block.scalar
        def _(act):
            signed = [0]

            def load_unit(u):
                act.dma_start(stage[:, u % STAGES, :], w_units[u // NC, u % NC]).then_inc(w_in[u % STAGES], DMA)

            def sign_units(until):
                for u in range(signed[0], until):
                    if 0 < u and u - 1 + STAGES < UNITS:
                        act.wait_ge(w_signed, u)
                        load_unit(u - 1 + STAGES)
                    act.wait_ge(w_in[u % STAGES], DMA * (u // STAGES + 1))
                    nc.scalar.activation(signs[:, u % NC, columns(u // NC)], stage[:, u % STAGES, :],
                                         ACT.Sign).then_inc(w_signed, 1)
                signed[0] = until

            def high(g, q, odd, ready, done):
                act.wait_ge(ready, NG * q + g + 1)
                nc.scalar.activation(hi[odd][:, group(g), :], y[:, group(g), :], ACT.Copy).then_inc(done, 1)

            def keep_bias(q):
                act.wait_ge(bias_mm, q + 1)
                nc.scalar.activation(bias_y[:, :], bias_sum, ACT.Copy).then_inc(bias_y_ready, 1)

            def route_exps(q):
                act.wait_ge(route_steps, 8 * q + 2)
                nc.scalar.activation(exps[:, :], logits[:, :], ACT.Exp, bias=top[:, :],
                                     accum_out=total[:, :]).then_inc(route_exp, 1)

            def keep_route(q, odd):
                act.wait_ge(route_mm, q + 1)
                nc.scalar.activation(routeT[odd][:, :], routeT_ps, ACT.Copy).then_inc(route_ready, 1)

            def keep_out_scale(b, n, first=False):
                act.wait_ge(out_scale_mm, NB * b + n + 1)
                if not first:
                    act.wait_ge(scaled, NB * b + n)
                nc.scalar.activation(out_scale[:, :], scale_bank[:, :], ACT.Copy).then_inc(out_scale_ready, 1)

            for u in range(STAGES):
                load_unit(u)
            act.wait_ge(smalls_in, DMA * SMALLS)
            act.wait_ge(hidden, 1)
            nc.scalar.activation(h1[:, :], ring[0][:, 0:B], ACT.Gelu, bias=b0c[:, :]).then_inc(gelu_done, 1)
            act.wait_ge(hidden, 2)
            nc.scalar.activation(h2[:, :], ring[1][:, 0:B], ACT.Gelu, bias=b1c[:, :]).then_inc(gelu_done, 1)
            act.wait_ge(att_steps, 2)
            nc.scalar.activation(exps[0:B, :], logits[0:B, :], ACT.Exp, bias=top[0:B, :],
                                 accum_out=total[0:B, :]).then_inc(att_exp, 1)
            sign_units(8)
            keep_bias(0)
            for g in range(NG):
                high(g, 0, 0, y_ready, y_hi)
                sign_units(10 + 2 * g)
            route_exps(0)
            sign_units(20)
            keep_route(0, 0)
            for g in range(NG):
                high(g, 0, 0, z_ready, z_hi)

            def step(b, pair, odd, more, early):
                q, nxt = b + 1, 1 - odd
                loading = early and odd == 0
                keep_out_scale(b, 0, first=loading)
                if loading:
                    sign_units(2 * NC)
                if more:
                    keep_bias(q)
                    for g in range(NG):
                        high(g, q, nxt, y_ready, y_hi)
                if loading:
                    sign_units(3 * NC)
                keep_out_scale(b, 1)
                if more:
                    route_exps(q)
                keep_out_scale(b, 2)
                if loading:
                    sign_units(4 * NC)
                if more:
                    keep_route(q, nxt)
                keep_out_scale(b, 3)
                if more:
                    for g in range(NG):
                        high(g, q, nxt, z_ready, z_hi)

            steps(act, step)

        @block.tensor
        def _(pe):
            def bias_product(q):
                pe.wait_ge(mixed_ready, q + 1)
                nc.tensor.matmul(bias_sum, ones[0:E, :], mixed_b[:, :], start=True, stop=True).then_inc(bias_mm, 1)

            def y_chunk(q, pair_q, odd, c, first=False):
                if c == 0:
                    pe.wait_ge(x_in[odd], DMA * NB * (pair_q + 1))
                    pe.wait_ge(mixed_ready, q + 1)
                g = c // GC
                if c % GC == 0 and not first:
                    pe.wait_ge(z_ready, NG * q - NG + g + 1)
                done = nc.tensor.matmul(ring[g][:, chunk(c % GC)], xs[odd][:, chunk(c)], mixed[:, :],
                                        start=True, stop=True)
                if c % GC == GC - 1:
                    done.then_inc(y_mm, 1)

            def gate_chunk(q, odd, c):
                if c % GC == 0:
                    pe.wait_ge(y_hi, NG * q + c // GC + 1)
                    pe.wait_ge(y_lo, NG * q + c // GC + 1)
                if c == 0:
                    pe.wait_ge(bias_y_ready, q + 1)
                for half, of in enumerate((hi, lo)):
                    done = nc.tensor.matmul(gate_sum, of[odd][:, c, :], gate[:, c, :],
                                            start=(c == 0 and half == 0), stop=(c == NC - 1 and half == 1))
                if c == NC - 1:
                    done.then_inc(gates_mm, 1)

            def route_transpose(q):
                pe.wait_ge(parts_ready, q + 1)
                nc.tensor.transpose(routeT_ps, parts[:, :, :, :].rearrange("p i j e -> p (i j e)"),
                                    unit[:, :]).then_inc(route_mm, 1)

            def in_scale_chunk(q, odd, c):
                g = c // GC
                if c == 0:
                    pe.wait_ge(route_ready, q + 1)
                if c % GC == 0:
                    pe.wait_ge(y_ready, NG * q + g + 1)
                done = nc.tensor.matmul(ring[g][:, chunk(c % GC)], in_stack[:, chunk(c)], routeT[odd][:, :],
                                        start=True, stop=True)
                if c % GC == GC - 1:
                    done.then_inc(scale_mm, 1)

            def out_scale_block(b, odd, n, first=False):
                if not first:
                    pe.wait_ge(out_scale_ready, NB * b + n)
                nc.tensor.matmul(scale_bank[:, :], routeT[odd][:, :], out_stack[:, columns(n)],
                                 start=True, stop=True).then_inc(out_scale_mm, 1)

            pe.wait_ge(smalls_in, DMA * SMALLS)
            nc.tensor.matmul(ring[0][:, 0:B], w0, emb[:, :], start=True, stop=True).then_inc(hidden, 1)
            pe.wait_ge(gelu_done, 1)
            nc.tensor.matmul(ring[1][:, 0:B], w1, h1[:, :], start=True, stop=True).then_inc(hidden, 1)
            pe.wait_ge(gelu_done, 2)
            nc.tensor.matmul(ring[2][0:B, 0:E], h2[:, :], w2[:, :], start=True, stop=True).then_inc(hidden, 1)
            pe.wait_ge(constants, 5)
            pe.wait_ge(att_steps, 5)
            nc.tensor.matmul(ring[3][:, 0:B * E], ones[0:B, :], att_wide[:, :, :].rearrange("b c e -> b (c e)"),
                             start=True, stop=True).then_inc(att_spread, 1)
            nc.tensor.matmul(ring[2][0:E, E:E + B], att[:, :], unit32[:, :], start=True, stop=True)\
              .then_inc(att_spread, 1)
            bias_product(0)
            for c in range(NC):
                y_chunk(0, 0, 0, c, first=True)
            pe.wait_ge(gate_cut, 2)
            for c in range(NC):
                gate_chunk(0, 0, c)
            route_transpose(0)
            pe.wait_ge(stacked, DMA * 2 * PARTS * PARTS)
            for c in range(NC):
                in_scale_chunk(0, 0, c)

            def step(b, pair, odd, more, early):
                q, nxt = b + 1, 1 - odd
                loading = early and odd == 0
                for m in range(NB * MM):
                    n, k, half = m // MM, m % MM // 2, m % 2
                    if m % MM == 0:
                        out_scale_block(b, odd, n, first=loading and n == 0)
                        if not (loading and n < 2):
                            pe.wait_ge(scaled, NB * b + n - 1)
                    if loading and half == 0:
                        pe.wait_ge(w_signed, n * NC + k + 1)
                    if n == 0 and half == 0 and k % GC == 0:
                        pe.wait_ge(z_hi, NG * b + k // GC + 1)
                        pe.wait_ge(z_lo, NG * b + k // GC + 1)
                    done = nc.tensor.matmul(main[n % 2][:, :], (hi, lo)[half][odd][:, k, :],
                                            signs[:, k, columns(n)],
                                            start=(m % MM == 0), stop=(m % MM == MM - 1))
                    if m % MM == MM - 1:
                        done.then_inc(main_mm, 1)
                    if not more:
                        continue
                    if m == BIAS_AT:
                        bias_product(q)
                    if m in range(Y_AT, Y_AT + 2 * NC, 2):
                        y_chunk(q, pair + odd, nxt, (m - Y_AT) // 2)
                    if m in range(GATE_AT, GATE_AT + 2 * NC, 2):
                        gate_chunk(q, nxt, (m - GATE_AT) // 2)
                    if m == ROUTE_AT:
                        route_transpose(q)
                    if m in range(SCALE_AT, SCALE_AT + NC):
                        in_scale_chunk(q, nxt, m - SCALE_AT)

            steps(pe, step)

        @block.vector
        def _(dve):
            def mix(q):
                nc.vector.tensor_copy(att_q[:, :], att_rows[:, bass.ds(q, 1), :].rearrange("p o e -> p (o e)"))\
                  .then_inc(mix_steps, 1)
                nc.vector.tensor_scalar(mixed_b[:, :], mix_b[:, :], attT[:, bass.ds(q, 1)], None,
                                        ALU.mult).then_inc(mix_steps, 1)
                dve.wait_ge(mix_steps, (E + 1) * q + 2)
                nc.vector.tensor_scalar(mixed[:, :], mix_w[:, 0, :], att_q[:, 0:1], None,
                                        ALU.mult).then_inc(mix_steps, 1)
                for k in range(1, E):
                    dve.wait_ge(mix_steps, (E + 1) * q + 2 + k)
                    done = nc.vector.scalar_tensor_tensor(mixed[:, :], mix_w[:, k, :], att_q[:, k:k + 1],
                                                          mixed[:, :], ALU.mult, ALU.add)
                    if k < E - 1:
                        done.then_inc(mix_steps, 1)
                done.then_inc(mixed_ready, 1)

            def y_sum(q, odd, g):
                dve.wait_ge(y_mm, NG * q + g + 1)
                if g == 0:
                    dve.wait_ge(bias_y_ready, q + 1)
                nc.vector.tensor_tensor(y[:, group(g), :], by_chunk(ring[g]),
                                        bias_y[:, :].unsqueeze(1).to_broadcast([P, GC, T]),
                                        ALU.add).then_inc(y_ready, 1)

            def low(q, odd, g, high_done, done):
                dve.wait_ge(high_done, NG * q + g + 1)
                nc.vector.tensor_tensor(lo[odd][:, group(g), :], y[:, group(g), :],
                                        hi[odd][:, group(g), :].bitcast(F32), ALU.subtract).then_inc(done, 1)

            def z_product(q, g):
                dve.wait_ge(scale_mm, NG * q + g + 1)
                nc.vector.tensor_tensor(y[:, group(g), :], y[:, group(g), :], by_chunk(ring[g]),
                                        ALU.mult).then_inc(z_ready, 1)

            def routing(q):
                dve.wait_ge(gates_mm, q + 1)
                nc.vector.tensor_reduce(logits[:, :], gate_sum.rearrange("t (h e) -> t e h", h=2), AX_X,
                                        ALU.add).then_inc(route_steps, 1)
                dve.wait_ge(route_steps, 8 * q + 1)
                nc.vector.tensor_reduce(top[:, :], logits[:, :], AX_X, ALU.max, negate=True)\
                  .then_inc(route_steps, 1)
                dve.wait_ge(route_exp, q + 1)
                nc.vector.reciprocal(inverse[:, :], total[:, :]).then_inc(route_steps, 1)
                dve.wait_ge(route_steps, 8 * q + 3)
                nc.vector.tensor_scalar(route[:, :], exps[:, :], inverse[:, :], None, ALU.mult)\
                  .then_inc(route_steps, 1)
                of = route[:, :]
                for i in range(PARTS):
                    dve.wait_ge(route_steps, 8 * q + 4 + 2 * i)
                    done = nc.vector.tensor_copy(parts[:, i, :, :], of.unsqueeze(1).to_broadcast([P, PARTS, E]))
                    if i == PARTS - 1:
                        done.then_inc(parts_ready, 1)
                        break
                    done.then_inc(route_steps, 1)
                    dve.wait_ge(route_steps, 8 * q + 5 + 2 * i)
                    nc.vector.tensor_tensor(rest[:, i, :], of, parts[:, i, 0, :], ALU.subtract)\
                      .then_inc(route_steps, 1)
                    of = rest[:, i, :]

            def finish(b, odd, n, pair, first=False):
                dve.wait_ge(main_mm, NB * b + n + 1)
                dve.wait_ge(out_scale_ready, NB * b + n + 1)
                if not first:
                    dve.wait_ge(stored[n % 2], DMA * (NB // 2 * b + n // 2))
                nc.vector.tensor_tensor(results[n % 2][:, :], main[n % 2][:, :], out_scale[:, :],
                                        ALU.mult).then_inc(scaled, 1)
                dve.wait_ge(x_biased, NB * b + n + 1)
                dve.wait_ge(scaled, NB * b + n + 1)
                nc.vector.tensor_tensor(results[n % 2][:, :], results[n % 2][:, :], xs[odd][:, columns(n)],
                                        ALU.add).then_inc(result_ready, 1)

            dve.wait_ge(smalls_in, DMA * SMALLS)
            dve.wait_ge(hidden, 3)
            nc.vector.tensor_tensor(logits[0:B, :], ring[2][0:B, 0:E], b2r[:, :], ALU.add).then_inc(att_steps, 1)
            dve.wait_ge(att_steps, 1)
            nc.vector.tensor_reduce(top[0:B, :], logits[0:B, :], AX_X, ALU.max, negate=True).then_inc(att_steps, 1)
            dve.wait_ge(att_exp, 1)
            nc.vector.reciprocal(inverse[0:B, :], total[0:B, :]).then_inc(att_steps, 1)
            dve.wait_ge(att_steps, 3)
            nc.vector.tensor_scalar(att[:, :], exps[0:B, :], inverse[0:B, :], None, ALU.mult).then_inc(att_steps, 1)
            dve.wait_ge(att_steps, 4)
            dve.wait_ge(constants, 5)
            nc.vector.tensor_tensor(att_wide[:, :, :], att[:, :].unsqueeze(1).to_broadcast([B, B, E]),
                                    unit32[:, :].unsqueeze(2).to_broadcast([B, B, E]), ALU.mult)\
              .then_inc(att_steps, 1)
            dve.wait_ge(att_spread, 2)
            nc.vector.tensor_copy(att_rows[:, :, :].rearrange("p b e -> p (b e)"), ring[3][:, 0:B * E])\
              .then_inc(att_kept, 1)
            nc.vector.tensor_copy(attT[:, :], ring[2][0:E, E:E + B]).then_inc(att_kept, 1)
            dve.wait_ge(att_kept, 2)
            dve.wait_ge(mixes_in, 2 * DMA)
            mix(0)

            def y_halves(q, odd):
                y_sum(q, odd, 0)
                for g in range(1, NG):
                    y_sum(q, odd, g)
                    low(q, odd, g - 1, y_hi, y_lo)
                low(q, odd, NG - 1, y_hi, y_lo)

            def z_halves(q, odd):
                z_product(q, 0)
                for g in range(1, NG):
                    z_product(q, g)
                    low(q, odd, g - 1, z_hi, z_lo)
                low(q, odd, NG - 1, z_hi, z_lo)

            y_halves(0, 0)
            routing(0)
            mix(1)
            z_halves(0, 0)

            def step(b, pair, odd, more, early):
                q, nxt = b + 1, 1 - odd
                last_prepared = isinstance(b, int) and b + 2 >= B
                if not (early and odd == 0):
                    finish(b - 1, nxt, NB - 1, pair)
                if more:
                    y_halves(q, nxt)
                finish(b, odd, 0, pair, first=early and odd == 0)
                finish(b, odd, 1, pair, first=early and odd == 0)
                if more:
                    routing(q)
                    if not last_prepared:
                        mix(q + 1)
                finish(b, odd, 2, pair)
                if more:
                    z_halves(q, nxt)
                if isinstance(b, int) and b == B - 1:
                    finish(b, odd, NB - 1, pair)

            steps(dve, step)


def kernel(**inputs):
    import numpy as np
    import concourse.bacc as bacc
    from concourse.bass_utils import run_bass_kernel_spmd

    a = {name: np.asarray(v) for name, v in inputs.items()}
    B, T, H = a["x"].shape
    E = a["L0_cond_W2"].shape[1]
    P_ = 128
    scales = np.stack([a["L0_ffn_in_channel_scale"].reshape(P_, -1), a["L0_ffn_out_channel_scale"].reshape(P_, -1)], 1)
    laid = {
        "x": a["x"],
        "embT": a["cond_128"].T,
        "W0": a["L0_cond_W0"],
        "b0": a["L0_cond_b0"][:, None],
        "W1": a["L0_cond_W1"],
        "b1": a["L0_cond_b1"][:, None],
        "W2": a["L0_cond_W2"],
        "b2": np.broadcast_to(a["L0_cond_b2"], (B, E)),
        "mixT": a["L0_cond_weight"][..., 0].transpose(2, 0, 1),
        "mix_bias": a["L0_cond_bias_k"],
        "ffn_wT": a["L0_ffn_weight"].T,
        "ffn_bias": a["L0_ffn_bias"],
        "gateT": a["L0_ffn_gate_w"].reshape(E, H // P_, P_).transpose(2, 1, 0),
        "scales": scales,
    }
    laid = {name: np.ascontiguousarray(v) for name, v in laid.items()}
    nc = bacc.Bacc("TRN2", target_bir_lowering=False, num_devices=1, dynamic_dma_scratch_size=1024)
    args = {name: nc.dram_tensor(f"in_{name}", v.shape, mybir.dt.from_np(v.dtype), kind="ExternalInput").ap()
            for name, v in laid.items()}
    out = nc.dram_tensor("out_0", (B, T, H), F32, kind="ExternalOutput").ap()
    adaln_ffn(nc, *args.values(), out)
    r = run_bass_kernel_spmd(nc, [{f"in_{name}": v for name, v in laid.items()}], core_ids=[0])
    return r.results[0]["out_0"]
```

```python
from contextlib import ExitStack

import concourse.bass as bass
from concourse import mybir

ALU = mybir.AluOpType
ACT = mybir.ActivationFunctionType
AX_X = mybir.AxisListType.X
F32 = mybir.dt.float32
F32R = mybir.dt.float32r
BF16 = mybir.dt.bfloat16

P = 128
NW = 512
PARTS = 3
DMA = 16
W_AHEAD = 3


def adaln_ffn(nc, x, embT, W0, b0, W1, b1, W2, b2, mixT, mix_bias, ffn_wT, ffn_bias, gateT, scales, out):
    B, T, H = x.shape
    E = W2.shape[1]
    NC = H // P
    NB = ffn_wT.shape[1] // NW
    GC = NW // P
    NG = NC // GC
    R = PARTS * PARTS * E
    SC = 2
    SPB = NC // SC
    HH = P // E
    MM = 2 * NC
    assert T == P and NG == NB and B % 2 == 0

    BIAS_AT = 0
    Y_AT = 4
    GATE_AT = 22
    FOLD_AT = 56
    ROUTE_AT = 76
    SCALE_AT = 80

    with ExitStack() as ctx:
        def sb(name, shape, dt=F32):
            return ctx.enter_context(nc.sbuf_tensor(name, shape, dt))

        def bank(name):
            return ctx.enter_context(nc.psum_tensor(name, [P, NW], F32))

        def sem(name):
            return ctx.enter_context(nc.semaphore(name))

        with nc.sbuf_tensor("w_loaded", [P, NB, NC, NW], F32) as w_loaded:
            pass
        signs = sb("signs", [P, NB, NC, NW], F32R)
        xs = [sb(f"xs{i}", [P, H]) for i in range(2)]
        y = sb("y", [P, NC, T])
        halves = [sb(f"halves{i}", [P, NC, 2, T], F32R) for i in range(2)]
        results = [sb(f"results{i}", [P, NW]) for i in range(2)]
        out_scale = sb("out_scale", [P, NW])
        bias_rows = sb("bias_rows", [P, NB * NW])
        in_stack = sb("in_stack", [R, H], BF16)
        out_stack = sb("out_stack", [R, NB * NW], BF16)
        mix_w = sb("mix_w", [P, E, P])
        mix_b = sb("mix_b", [E, P])
        mixed = sb("mixed", [P, P])
        mixed_b = sb("mixed_b", [E, P])
        bias_y = sb("bias_y", [P, T])
        gate = sb("gate", [P, NC * 2 * E + P - 2 * E], F32R)
        gate_halves = gate[:, 0:NC * 2 * E].rearrange("p (c h e) -> p c h e", h=2, e=E)
        gate_parts = sb("gate_parts", [2 * E, 2, T])
        fold = sb("fold", [2 * E, E])
        att_rows = sb("att_rows", [P, B, E])
        att_q = sb("att_q", [P, E])
        attT = sb("attT", [E, B])
        logits = sb("logits", [B, E])
        top = sb("top", [P, 1])
        exps = sb("exps", [P, E])
        total = sb("total", [P, 1])
        inverse = sb("inverse", [P, 1])
        route = sb("route", [P, E])
        rest = sb("rest", [P, 2, E])
        parts = sb("parts", [P, PARTS, PARTS, E], BF16)
        routeT = [sb(f"routeT{i}", [R, T], BF16) for i in range(2)]
        ones = sb("ones", [32, P])
        unit32 = sb("unit32", [32, 32])
        unit = sb("unit", [P, P], BF16)
        emb = sb("emb", [P, B])
        w0 = results[0][:, 0:P]
        w1 = results[0][:, P:2 * P]
        att_wide = results[0][0:B, 2 * P:2 * P + B * E].rearrange("b (c e) -> b c e", e=E)
        cut_in = results[1][:, 0:2 * P].rearrange("p (s f) -> p s f", s=2)
        cut_rest = results[1][:, 2 * P:4 * P].rearrange("p (s f) -> p s f", s=2)
        gate_in = out_scale[:, PARTS * P:4 * P].rearrange("p (c e) -> p c e", e=E)
        cuts = out_scale[:, 0:PARTS * P].bitcast(BF16).rearrange("p (j s f) -> p j s f", j=PARTS, s=2)
        w2 = sb("w2", [P, E])
        b0c = sb("b0c", [P, 1])
        b1c = sb("b1c", [P, 1])
        b2r = sb("b2r", [B, E])
        h1 = sb("h1", [P, B])
        h2 = sb("h2", [P, B])
        att = sb("att", [B, E])

        main = [bank(f"main{i}") for i in range(2)]
        ring = [bank(f"ring{g}") for g in range(NG)]
        scale_bank = bank("scale_bank")
        small = bank("small")
        gate_sum = small[:, 0:2 * T]
        bias_sum = small[:, 2 * T:3 * T]
        route_logits = small[:, 3 * T:3 * T + E]
        routeT_ps = small[0:R, 3 * T + T // 2:4 * T].bitcast(BF16)

        smalls_in = sem("smalls_in")
        mixes_in = sem("mixes_in")
        gates_in = sem("gates_in")
        bias_in = sem("bias_in")
        x_in = [[sem(f"x_in{i}_{n}") for n in range(NB)] for i in range(2)]
        w_in = [sem(f"w_in{i}") for i in range(NB * NG)]
        w_signed = sem("w_signed")
        constants = sem("constants")
        cut_steps = sem("cut_steps")
        stacked = sem("stacked")
        gate_cut = sem("gate_cut")
        hidden = sem("hidden")
        gelu_done = sem("gelu_done")
        att_steps = sem("att_steps")
        att_exp = sem("att_exp")
        att_spread = sem("att_spread")
        att_kept = sem("att_kept")
        mix_steps = sem("mix_steps")
        mixed_ready = sem("mixed_ready")
        bias_mm = sem("bias_mm")
        bias_y_ready = sem("bias_y_ready")
        y_mm = sem("y_mm")
        y_ready = sem("y_ready")
        y_hi = sem("y_hi")
        y_lo = sem("y_lo")
        gates_mm = sem("gates_mm")
        gate_parts_ready = sem("gate_parts_ready")
        logits_mm = sem("logits_mm")
        route_steps = sem("route_steps")
        route_exp = sem("route_exp")
        parts_ready = sem("parts_ready")
        route_mm = sem("route_mm")
        route_ready = sem("route_ready")
        scale_mm = sem("scale_mm")
        z_ready = sem("z_ready")
        z_hi = sem("z_hi")
        z_lo = sem("z_lo")
        out_scale_mm = sem("out_scale_mm")
        out_scale_ready = sem("out_scale_ready")
        main_mm = sem("main_mm")
        scaled = sem("scaled")
        result_ready = sem("result_ready")
        x_biased = sem("x_biased")
        stored = [sem(f"stored{i}") for i in range(2)]

        block = ctx.enter_context(nc.Block())

        def chunk(c):
            return slice(c * P, (c + 1) * P)

        def columns(n):
            return slice(n * NW, (n + 1) * NW)

        def group(g):
            return slice(g * GC, (g + 1) * GC)

        def by_chunk(b):
            return b[:, :].rearrange("p (c t) -> p c t", c=GC)

        def steps(engine, step):
            for b in range(2):
                step(b, 0, b, True, True)
            with engine.Fori(1, B // 2 - 1) as pair:
                for odd in range(2):
                    step(2 * pair + odd, pair, odd, True, False)
            for b in (B - 2, B - 1):
                step(b, B // 2 - 1, b % 2, b + 1 < B, False)

        SMALLS = 7
        w_pieces = ffn_wT.rearrange("(g c p) (n w) -> n g p c w", p=P, c=GC, w=NW)

        @block.sync
        def _(sp):
            for dst, src in ((emb[:, :], embT), (w0, W0), (b0c[:, :], b0), (w1, W1), (b1c[:, :], b1), (w2[:, :], W2)):
                sp.dma_start(dst, src).then_inc(smalls_in, DMA)
            sp.dma_start(b2r[:, :], b2).then_inc(smalls_in, DMA)
            sp.dma_start(mix_w[:, :, :], mixT).then_inc(mixes_in, DMA)
            sp.dma_start(mix_b[:, :], mix_bias).then_inc(mixes_in, DMA)
            for n in range(NB):
                sp.dma_start(xs[0][:, columns(n)], x[0, :, columns(n)]).then_inc(x_in[0][n], DMA)
            sp.dma_start(gate_in[:, :, :], gateT).then_inc(gates_in, DMA)
            sp.dma_start(cut_in[:, :, :], scales).then_inc(gates_in, DMA)
            for u in range(NB * NG):
                if u >= W_AHEAD:
                    sp.wait_ge(w_in[u - W_AHEAD], DMA)
                n, g = u // NG, u % NG
                sp.dma_start(w_loaded[:, n, group(g), :], w_pieces[n, g]).then_inc(w_in[u], DMA)
                if u == W_AHEAD - 1:
                    sp.wait_ge(cut_steps, 5)
                    for i in range(PARTS):
                        for j in range(PARTS):
                            for s, stack in enumerate((in_stack, out_stack)):
                                row = (PARTS * i + j) * E
                                sp.dma_start(stack[row:row + E, :].rearrange("e (h f) -> e h f", f=P),
                                             cuts[:, j, s, :]).then_inc(stacked, DMA)
                if u == NG:
                    for n in range(NB):
                        sp.dma_start(xs[1][:, columns(n)], x[1, :, columns(n)]).then_inc(x_in[1][n], DMA)
                if u == NG + 1:
                    sp.dma_start(bias_rows[:, :], ffn_bias.partition_broadcast(P)).then_inc(bias_in, DMA)

            def step(b, pair, odd, more, early):
                for n in range(NB):
                    sp.wait_ge(result_ready, NB * b + n + 1)
                    sp.dma_start(out[bass.ds(b, 1), :, columns(n)].rearrange("o p w -> (o p) w"),
                                 results[n % 2][:, :]).then_inc(stored[n % 2], DMA)
                    if isinstance(b, int) and b + 2 >= B:
                        continue
                    sp.dma_start(xs[odd][:, columns(n)],
                                 x[bass.ds(b + 2, 1), :, columns(n)].rearrange("o p w -> (o p) w"))\
                      .then_inc(x_in[odd][n], DMA)

            steps(sp, step)
            for i in range(2):
                sp.wait_ge(stored[i], DMA * B * NB // 2)

        @block.gpsimd
        def _(pool):
            nc.gpsimd.memset(unit32[:, :], 0.0).then_inc(constants, 1)
            nc.gpsimd.memset(unit[:, :], 0.0).then_inc(constants, 1)
            nc.gpsimd.memset(fold[:, :], 0.0).then_inc(constants, 1)
            nc.gpsimd.memset(ones[:, :], 1.0).then_inc(constants, 1)
            nc.gpsimd.memset(gate[:, NC * 2 * E:].bitcast(F32), 0.0).then_inc(constants, 1)
            pool.wait_ge(constants, 5)
            for m, n, base in ((unit32, 32, 0), (unit, P, 0), (fold, E, 0), (fold, E, -E)):
                if base:
                    pool.wait_ge(constants, 8)
                nc.gpsimd.affine_select(out=m[:, :], in_=m[:, :], compare_op=ALU.not_equal, fill=1.0,
                                        base=base, pattern=[[-1, n]], channel_multiplier=1).then_inc(constants, 1)
            pool.wait_ge(gates_in, 2 * DMA)
            nc.gpsimd.tensor_copy(gate_halves[:, :, 0, :], gate_in[:, :, :]).then_inc(gate_cut, 1)
            nc.gpsimd.tensor_copy(cuts[:, 0, :, :], cut_in[:, :, :]).then_inc(cut_steps, 1)
            pool.wait_ge(gate_cut, 1)
            nc.gpsimd.tensor_tensor(gate_halves[:, :, 1, :], gate_in[:, :, :], gate_halves[:, :, 0, :].bitcast(F32),
                                    ALU.subtract).then_inc(gate_cut, 1)
            pool.wait_ge(cut_steps, 1)
            nc.gpsimd.tensor_tensor(cut_rest[:, :, :], cut_in[:, :, :], cuts[:, 0, :, :],
                                    ALU.subtract).then_inc(cut_steps, 1)
            pool.wait_ge(cut_steps, 2)
            nc.gpsimd.tensor_copy(cuts[:, 1, :, :], cut_rest[:, :, :]).then_inc(cut_steps, 1)
            pool.wait_ge(cut_steps, 3)
            nc.gpsimd.tensor_tensor(cut_rest[:, :, :], cut_rest[:, :, :], cuts[:, 1, :, :],
                                    ALU.subtract).then_inc(cut_steps, 1)
            pool.wait_ge(cut_steps, 4)
            nc.gpsimd.tensor_copy(cuts[:, 2, :, :], cut_rest[:, :, :]).then_inc(cut_steps, 1)

            def add_bias(q, odd):
                pool.wait_ge(y_mm, NG * q + NG)
                for n in range(NB):
                    nc.gpsimd.tensor_tensor(xs[odd][:, columns(n)], xs[odd][:, columns(n)],
                                            bias_rows[:, columns(n)], ALU.add).then_inc(x_biased, 1)

            pool.wait_ge(bias_in, DMA)
            add_bias(0, 0)

            def step(b, pair, odd, more, early):
                if more:
                    add_bias(b + 1, 1 - odd)

            steps(pool, step)

        @block.scalar
        def _(act):
            signed = [0]

            def sign_pieces(until):
                for u in range(signed[0], until):
                    n, c = u // SPB, u % SPB * SC
                    if c % GC == 0:
                        act.wait_ge(w_in[NG * n + c // GC], DMA)
                    nc.scalar.activation(signs[:, n, c:c + SC, :], w_loaded[:, n, c:c + SC, :],
                                         ACT.Sign).then_inc(w_signed, 1)
                signed[0] = until

            def high(g, q, odd, ready, done):
                act.wait_ge(ready, NG * q + g + 1)
                nc.scalar.activation(halves[odd][:, group(g), 0, :], y[:, group(g), :], ACT.Copy).then_inc(done, 1)

            def keep_bias(q):
                act.wait_ge(bias_mm, q + 1)
                nc.scalar.activation(bias_y[:, :], bias_sum, ACT.Copy).then_inc(bias_y_ready, 1)

            def keep_gate_parts(q):
                act.wait_ge(gates_mm, q + 1)
                nc.scalar.activation(gate_parts[:, :, :].rearrange("r h t -> r (h t)"), gate_sum[0:2 * E, :],
                                     ACT.Copy).then_inc(gate_parts_ready, 1)

            def route_exps(q):
                act.wait_ge(route_steps, 7 * q + 1)
                nc.scalar.activation(exps[:, :], route_logits, ACT.Exp, bias=top[:, :],
                                     accum_out=total[:, :]).then_inc(route_exp, 1)

            def keep_route(q, odd):
                act.wait_ge(route_mm, q + 1)
                nc.scalar.activation(routeT[odd][:, :], routeT_ps, ACT.Copy).then_inc(route_ready, 1)

            def keep_out_scale(b, n, first=False):
                act.wait_ge(out_scale_mm, NB * b + n + 1)
                if not first:
                    act.wait_ge(scaled, NB * b + n)
                nc.scalar.activation(out_scale[:, :], scale_bank[:, :], ACT.Copy).then_inc(out_scale_ready, 1)

            act.wait_ge(smalls_in, DMA * SMALLS)
            act.wait_ge(hidden, 1)
            nc.scalar.activation(h1[:, :], ring[0][:, 0:B], ACT.Gelu, bias=b0c[:, :]).then_inc(gelu_done, 1)
            act.wait_ge(hidden, 2)
            nc.scalar.activation(h2[:, :], ring[1][:, 0:B], ACT.Gelu, bias=b1c[:, :]).then_inc(gelu_done, 1)
            act.wait_ge(att_steps, 2)
            nc.scalar.activation(exps[0:B, :], logits[:, :], ACT.Exp, bias=top[0:B, :],
                                 accum_out=total[0:B, :]).then_inc(att_exp, 1)
            sign_pieces(2)
            keep_bias(0)
            for g in range(NG):
                high(g, 0, 0, y_ready, y_hi)
                sign_pieces(3 + g)
            keep_gate_parts(0)
            route_exps(0)
            sign_pieces(SPB)
            keep_route(0, 0)
            for g in range(NG):
                high(g, 0, 0, z_ready, z_hi)

            def step(b, pair, odd, more, early):
                q, nxt = b + 1, 1 - odd
                loading = early and odd == 0
                keep_out_scale(b, 0, first=loading)
                if more:
                    keep_bias(q)
                    for g in range(NG):
                        high(g, q, nxt, y_ready, y_hi)
                        if loading:
                            sign_pieces(SPB + 2 + 2 * g)
                keep_out_scale(b, 1)
                if more:
                    keep_gate_parts(q)
                    route_exps(q)
                if loading:
                    sign_pieces(3 * SPB)
                if more:
                    keep_route(q, nxt)
                keep_out_scale(b, 2)
                if loading:
                    sign_pieces(4 * SPB)
                if more:
                    for g in range(NG):
                        high(g, q, nxt, z_ready, z_hi)
                keep_out_scale(b, 3)

            steps(act, step)

        @block.tensor
        def _(pe):
            def bias_product(q):
                pe.wait_ge(mixed_ready, q + 1)
                nc.tensor.matmul(bias_sum, ones[0:E, :], mixed_b[:, :], start=True, stop=True).then_inc(bias_mm, 1)

            def y_chunk(q, pair_q, odd, c, first=False):
                if c == 0:
                    pe.wait_ge(mixed_ready, q + 1)
                g = c // GC
                if c % GC == 0:
                    pe.wait_ge(x_in[odd][g], DMA * (pair_q + 1))
                if c % GC == 0 and not first:
                    pe.wait_ge(z_ready, NG * q - NG + g + 1)
                done = nc.tensor.matmul(ring[g][:, chunk(c % GC)], xs[odd][:, chunk(c)], mixed[:, :],
                                        start=True, stop=True)
                if c % GC == GC - 1:
                    done.then_inc(y_mm, 1)

            def gate_chunk(q, odd, c):
                if c % GC == 0:
                    pe.wait_ge(y_hi, NG * q + c // GC + 1)
                    pe.wait_ge(y_lo, NG * q + c // GC + 1)
                if c == 0:
                    pe.wait_ge(bias_y_ready, q + 1)
                done = nc.tensor.matmul(gate_sum, gate[:, 2 * E * c:2 * E * c + P],
                                        halves[odd][:, c, :, :].rearrange("p h t -> p (h t)"),
                                        start=(c == 0), stop=(c == NC - 1))
                if c == NC - 1:
                    done.then_inc(gates_mm, 1)

            def gate_fold(q):
                pe.wait_ge(gate_parts_ready, q + 1)
                for half in range(2):
                    done = nc.tensor.matmul(route_logits, gate_parts[:, half, :], fold[:, :],
                                            start=(half == 0), stop=(half == 1))
                done.then_inc(logits_mm, 1)

            def route_transpose(q):
                pe.wait_ge(parts_ready, q + 1)
                nc.tensor.transpose(routeT_ps, parts[:, :, :, :].rearrange("p i j e -> p (i j e)"),
                                    unit[:, :]).then_inc(route_mm, 1)

            def in_scale_chunk(q, odd, c):
                g = c // GC
                if c == 0:
                    pe.wait_ge(route_ready, q + 1)
                if c % GC == 0:
                    pe.wait_ge(y_ready, NG * q + g + 1)
                done = nc.tensor.matmul(ring[g][:, chunk(c % GC)], in_stack[:, chunk(c)], routeT[odd][:, :],
                                        start=True, stop=True)
                if c % GC == GC - 1:
                    done.then_inc(scale_mm, 1)

            def out_scale_block(b, odd, n, first=False):
                if not first:
                    pe.wait_ge(out_scale_ready, NB * b + n)
                nc.tensor.matmul(scale_bank[:, :], routeT[odd][:, :], out_stack[:, columns(n)],
                                 start=True, stop=True).then_inc(out_scale_mm, 1)

            pe.wait_ge(smalls_in, DMA * SMALLS)
            nc.tensor.matmul(ring[0][:, 0:B], w0, emb[:, :], start=True, stop=True).then_inc(hidden, 1)
            pe.wait_ge(gelu_done, 1)
            nc.tensor.matmul(ring[1][:, 0:B], w1, h1[:, :], start=True, stop=True).then_inc(hidden, 1)
            pe.wait_ge(gelu_done, 2)
            nc.tensor.matmul(ring[2][0:B, 0:E], h2[:, :], w2[:, :], start=True, stop=True).then_inc(hidden, 1)
            pe.wait_ge(constants, 9)
            pe.wait_ge(att_steps, 5)
            nc.tensor.matmul(ring[3][:, 0:B * E], ones[0:B, :], att_wide[:, :, :].rearrange("b c e -> b (c e)"),
                             start=True, stop=True).then_inc(att_spread, 1)
            nc.tensor.matmul(ring[2][0:E, E:E + B], att[:, :], unit32[:, :], start=True, stop=True)\
              .then_inc(att_spread, 1)
            bias_product(0)
            for c in range(NC):
                y_chunk(0, 0, 0, c, first=True)
            pe.wait_ge(gate_cut, 2)
            for c in range(NC):
                gate_chunk(0, 0, c)
            gate_fold(0)
            route_transpose(0)
            pe.wait_ge(stacked, DMA * 2 * PARTS * PARTS)
            for c in range(NC):
                in_scale_chunk(0, 0, c)

            def step(b, pair, odd, more, early):
                q, nxt = b + 1, 1 - odd
                loading = early and odd == 0
                for m in range(NB * MM):
                    n, k, half = m // MM, m % MM // 2, m % 2
                    if m % MM == 0:
                        out_scale_block(b, odd, n, first=loading and n == 0)
                        if not (loading and n < 2):
                            pe.wait_ge(scaled, NB * b + n - 1)
                    if loading and half == 0 and k % SC == 0:
                        pe.wait_ge(w_signed, n * SPB + k // SC + 1)
                    if n == 0 and half == 0 and k % GC == 0:
                        pe.wait_ge(z_hi, NG * b + k // GC + 1)
                        pe.wait_ge(z_lo, NG * b + k // GC + 1)
                    done = nc.tensor.matmul(main[n % 2][:, :], halves[odd][:, k, half, :],
                                            signs[:, n, k, :],
                                            start=(m % MM == 0), stop=(m % MM == MM - 1))
                    if m % MM == MM - 1:
                        done.then_inc(main_mm, 1)
                    if not more:
                        continue
                    if m == BIAS_AT:
                        bias_product(q)
                    if m in range(Y_AT, Y_AT + 2 * NC, 2):
                        y_chunk(q, pair + odd, nxt, (m - Y_AT) // 2)
                    if m in range(GATE_AT, GATE_AT + 2 * NC, 2):
                        gate_chunk(q, nxt, (m - GATE_AT) // 2)
                    if m == FOLD_AT:
                        gate_fold(q)
                    if m == ROUTE_AT:
                        route_transpose(q)
                    if m in range(SCALE_AT, SCALE_AT + NC):
                        in_scale_chunk(q, nxt, m - SCALE_AT)

            steps(pe, step)

        @block.vector
        def _(dve):
            def mix(q):
                nc.vector.tensor_copy(att_q[:, :], att_rows[:, bass.ds(q, 1), :].rearrange("p o e -> p (o e)"))\
                  .then_inc(mix_steps, 1)
                nc.vector.tensor_scalar(mixed_b[:, :], mix_b[:, :], attT[:, bass.ds(q, 1)], None,
                                        ALU.mult).then_inc(mix_steps, 1)
                dve.wait_ge(mix_steps, (E + 1) * q + 2)
                nc.vector.tensor_scalar(mixed[:, :], mix_w[:, 0, :], att_q[:, 0:1], None,
                                        ALU.mult).then_inc(mix_steps, 1)
                for k in range(1, E):
                    dve.wait_ge(mix_steps, (E + 1) * q + 2 + k)
                    done = nc.vector.scalar_tensor_tensor(mixed[:, :], mix_w[:, k, :], att_q[:, k:k + 1],
                                                          mixed[:, :], ALU.mult, ALU.add)
                    if k < E - 1:
                        done.then_inc(mix_steps, 1)
                done.then_inc(mixed_ready, 1)

            def y_sum(q, odd, g):
                dve.wait_ge(y_mm, NG * q + g + 1)
                if g == 0:
                    dve.wait_ge(bias_y_ready, q + 1)
                nc.vector.tensor_tensor(y[:, group(g), :], by_chunk(ring[g]),
                                        bias_y[:, :].unsqueeze(1).to_broadcast([P, GC, T]),
                                        ALU.add).then_inc(y_ready, 1)

            def low(q, odd, g, high_done, done):
                dve.wait_ge(high_done, NG * q + g + 1)
                nc.vector.tensor_tensor(halves[odd][:, group(g), 1, :], y[:, group(g), :],
                                        halves[odd][:, group(g), 0, :].bitcast(F32), ALU.subtract).then_inc(done, 1)

            def z_product(q, g):
                dve.wait_ge(scale_mm, NG * q + g + 1)
                nc.vector.tensor_tensor(y[:, group(g), :], y[:, group(g), :], by_chunk(ring[g]),
                                        ALU.mult).then_inc(z_ready, 1)

            def routing(q):
                dve.wait_ge(logits_mm, q + 1)
                nc.vector.tensor_reduce(top[:, :], route_logits, AX_X, ALU.max, negate=True)\
                  .then_inc(route_steps, 1)
                dve.wait_ge(route_exp, q + 1)
                nc.vector.reciprocal(inverse[:, :], total[:, :]).then_inc(route_steps, 1)
                dve.wait_ge(route_steps, 7 * q + 2)
                nc.vector.tensor_scalar(route[:, :], exps[:, :], inverse[:, :], None, ALU.mult)\
                  .then_inc(route_steps, 1)
                of = route[:, :]
                for i in range(PARTS):
                    dve.wait_ge(route_steps, 7 * q + 3 + 2 * i)
                    done = nc.vector.tensor_copy(parts[:, i, :, :], of.unsqueeze(1).to_broadcast([P, PARTS, E]))
                    if i == PARTS - 1:
                        done.then_inc(parts_ready, 1)
                        break
                    done.then_inc(route_steps, 1)
                    dve.wait_ge(route_steps, 7 * q + 4 + 2 * i)
                    nc.vector.tensor_tensor(rest[:, i, :], of, parts[:, i, 0, :], ALU.subtract)\
                      .then_inc(route_steps, 1)
                    of = rest[:, i, :]

            def finish(b, odd, n, pair, first=False):
                dve.wait_ge(main_mm, NB * b + n + 1)
                dve.wait_ge(out_scale_ready, NB * b + n + 1)
                if not first:
                    dve.wait_ge(stored[n % 2], DMA * (NB // 2 * b + n // 2))
                nc.vector.tensor_tensor(results[n % 2][:, :], main[n % 2][:, :], out_scale[:, :],
                                        ALU.mult).then_inc(scaled, 1)
                dve.wait_ge(x_biased, NB * b + n + 1)
                dve.wait_ge(scaled, NB * b + n + 1)
                nc.vector.tensor_tensor(results[n % 2][:, :], results[n % 2][:, :], xs[odd][:, columns(n)],
                                        ALU.add).then_inc(result_ready, 1)

            dve.wait_ge(smalls_in, DMA * SMALLS)
            dve.wait_ge(hidden, 3)
            nc.vector.tensor_tensor(logits[:, :], ring[2][0:B, 0:E], b2r[:, :], ALU.add).then_inc(att_steps, 1)
            dve.wait_ge(att_steps, 1)
            nc.vector.tensor_reduce(top[0:B, :], logits[:, :], AX_X, ALU.max, negate=True).then_inc(att_steps, 1)
            dve.wait_ge(att_exp, 1)
            nc.vector.reciprocal(inverse[0:B, :], total[0:B, :]).then_inc(att_steps, 1)
            dve.wait_ge(att_steps, 3)
            nc.vector.tensor_scalar(att[:, :], exps[0:B, :], inverse[0:B, :], None, ALU.mult).then_inc(att_steps, 1)
            dve.wait_ge(att_steps, 4)
            dve.wait_ge(constants, 9)
            nc.vector.tensor_tensor(att_wide[:, :, :], att[:, :].unsqueeze(1).to_broadcast([B, B, E]),
                                    unit32[:, :].unsqueeze(2).to_broadcast([B, B, E]), ALU.mult)\
              .then_inc(att_steps, 1)
            dve.wait_ge(att_spread, 2)
            nc.vector.tensor_copy(att_rows[:, :, :].rearrange("p b e -> p (b e)"), ring[3][:, 0:B * E])\
              .then_inc(att_kept, 1)
            nc.vector.tensor_copy(attT[:, :], ring[2][0:E, E:E + B]).then_inc(att_kept, 1)
            dve.wait_ge(att_kept, 2)
            dve.wait_ge(mixes_in, 2 * DMA)
            mix(0)

            def y_halves(q, odd):
                y_sum(q, odd, 0)
                for g in range(1, NG):
                    y_sum(q, odd, g)
                    low(q, odd, g - 1, y_hi, y_lo)
                low(q, odd, NG - 1, y_hi, y_lo)

            def z_halves(q, odd):
                z_product(q, 0)
                for g in range(1, NG):
                    z_product(q, g)
                    low(q, odd, g - 1, z_hi, z_lo)
                low(q, odd, NG - 1, z_hi, z_lo)

            y_halves(0, 0)
            routing(0)
            mix(1)
            z_halves(0, 0)

            def step(b, pair, odd, more, early):
                q, nxt = b + 1, 1 - odd
                last_prepared = isinstance(b, int) and b + 2 >= B
                if not (early and odd == 0):
                    finish(b - 1, nxt, NB - 1, pair)
                if more:
                    y_halves(q, nxt)
                finish(b, odd, 0, pair, first=early and odd == 0)
                if more:
                    routing(q)
                finish(b, odd, 1, pair, first=early and odd == 0)
                if more:
                    if not last_prepared:
                        mix(q + 1)
                    z_halves(q, nxt)
                finish(b, odd, 2, pair)
                if isinstance(b, int) and b == B - 1:
                    finish(b, odd, NB - 1, pair)

            steps(dve, step)


def kernel(**inputs):
    import numpy as np
    import concourse.bacc as bacc
    from concourse.bass_utils import run_bass_kernel_spmd

    a = {name: np.asarray(v) for name, v in inputs.items()}
    B, T, H = a["x"].shape
    E = a["L0_cond_W2"].shape[1]
    P_ = 128
    scales = np.stack([a["L0_ffn_in_channel_scale"].reshape(P_, -1), a["L0_ffn_out_channel_scale"].reshape(P_, -1)], 1)
    laid = {
        "x": a["x"],
        "embT": a["cond_128"].T,
        "W0": a["L0_cond_W0"],
        "b0": a["L0_cond_b0"][:, None],
        "W1": a["L0_cond_W1"],
        "b1": a["L0_cond_b1"][:, None],
        "W2": a["L0_cond_W2"],
        "b2": np.broadcast_to(a["L0_cond_b2"], (B, E)),
        "mixT": a["L0_cond_weight"][..., 0].transpose(2, 0, 1),
        "mix_bias": a["L0_cond_bias_k"],
        "ffn_wT": a["L0_ffn_weight"].T,
        "ffn_bias": a["L0_ffn_bias"],
        "gateT": a["L0_ffn_gate_w"].reshape(E, H // P_, P_).transpose(2, 1, 0),
        "scales": scales,
    }
    laid = {name: np.ascontiguousarray(v) for name, v in laid.items()}
    nc = bacc.Bacc("TRN2", target_bir_lowering=False, num_devices=1, dynamic_dma_scratch_size=1024)
    args = {name: nc.dram_tensor(f"in_{name}", v.shape, mybir.dt.from_np(v.dtype), kind="ExternalInput").ap()
            for name, v in laid.items()}
    out = nc.dram_tensor("out_0", (B, T, H), F32, kind="ExternalOutput").ap()
    adaln_ffn(nc, *args.values(), out)
    r = run_bass_kernel_spmd(nc, [{f"in_{name}": v for name, v in laid.items()}], core_ids=[0])
    return r.results[0]["out_0"]
```

```python
from contextlib import ExitStack

import numpy as np

import concourse.bass as bass
from concourse import mybir

ALU = mybir.AluOpType
ACT = mybir.ActivationFunctionType
AX_X = mybir.AxisListType.X
F32 = mybir.dt.float32
F32R = mybir.dt.float32r
BF16 = mybir.dt.bfloat16

P = 128
NW = 512
PARTS = 3
DMA = 16
WARM_UP = 48
W_AHEAD = 3


def adaln_ffn(nc, x, mlp, mixT, ffn_wT, ffn_bias, gate_scales, out):
    B, T, H = x.shape
    E = mixT.shape[1]
    NC = H // P
    NB = ffn_wT.shape[1] // NW
    GC = NW // P
    NG = NC // GC
    R = PARTS * PARTS * E
    SC = 2
    SPB = NC // SC
    HH = P // E
    MM = 2 * NC
    assert T == P and HH == NC and H == NB * NW and NG == NB and B % 2 == 0

    BIAS_AT = 0
    Y_AT = 4
    GATE_AT = 44
    FOLD_AT = 48
    ROUTE_AT = 66
    SCALE_AT = 76

    with ExitStack() as ctx:
        def sb(name, shape, dt=F32):
            return ctx.enter_context(nc.sbuf_tensor(name, shape, dt))

        def bank(name):
            return ctx.enter_context(nc.psum_tensor(name, [P, NW], F32))

        def sem(name):
            return ctx.enter_context(nc.semaphore(name))

        with nc.sbuf_tensor("w_loaded", [P, NB, NC, NW], F32) as w_loaded:
            pass
        signs = sb("signs", [P, NB, NC, NW], F32R)
        xs = [sb(f"xs{i}", [P, H]) for i in range(2)]
        y = sb("y", [P, NC, T])
        halves = [sb(f"halves{i}", [P, NC, 2, T], F32R) for i in range(2)]
        results = [sb(f"results{i}", [P, NW]) for i in range(2)]
        out_scale = sb("out_scale", [P, NW])
        bias_rows = sb("bias_rows", [P, NB * NW])
        stack = sb("stack", [R, HH, 2, P], BF16)
        mix_w = sb("mix_w", [P, E, P])
        mixed = sb("mixed", [P, P])
        mixed_b = sb("mixed_b", [P, P])
        bias_y = sb("bias_y", [P, T])
        gate = sb("gate", [P, NC * E + P // GC - E])
        gate_parts = sb("gate_parts", [P, T])
        fold = sb("fold", [P, E])
        att_rows = sb("att_rows", [P, B, E])
        att_q = sb("att_q", [P, E])
        attT = sb("attT", [E, B])
        logits = sb("logits", [B, E])
        top = sb("top", [P, 1])
        exps = sb("exps", [P, E])
        total = sb("total", [P, 1])
        inverse = sb("inverse", [P, 1])
        route = sb("route", [P, E])
        rest = sb("rest", [P, 2, E])
        parts = sb("parts", [P, PARTS, PARTS, E], BF16)
        routeT = [sb(f"routeT{i}", [R, T], BF16) for i in range(2)]
        ones = sb("ones", [P, P])
        unit32 = sb("unit32", [32, 32])
        unit = sb("unit", [P, P], BF16)
        h1 = sb("h1", [P, B])
        h2 = sb("h2", [P, B])
        att = sb("att", [B, E])
        warm = sb("warm", [1, 1])
        mlp_in = sb("mlp_in", list(mlp.shape))
        ends = np.cumsum([0, B, P, P, E, 1, 1, E, P])
        emb, w0, w1, w2, b0c, b1c, b2r, mix_b = (mlp_in[0:rows, ends[i]:ends[i + 1]]
                                                 for i, rows in enumerate((P, P, P, P, P, P, B, E)))
        gate_scales_in = sb("gate_scales_in", [P, 3 * P])
        cut_in = gate_scales_in[:, P:3 * P].rearrange("p (s f) -> p s f", s=2)
        att_wide = results[0][0:B, 0:B * E].rearrange("b (c e) -> b c e", e=E)
        cut_rest = results[1][:, 0:2 * P].rearrange("p (s f) -> p s f", s=2)
        cuts = out_scale[:, 0:PARTS * P].bitcast(BF16).rearrange("p (j s f) -> p j s f", j=PARTS, s=2)

        main = [bank(f"main{i}") for i in range(2)]
        ring = [bank(f"ring{g}") for g in range(NG)]
        scale_bank = bank("scale_bank")
        small = bank("small")
        gate_sum = small[:, 0:T]
        bias_sum = small[:, 2 * T:3 * T]
        route_logits = small[:, 3 * T:3 * T + E]
        routeT_ps = small[0:R, 3 * T + T // 2:4 * T].bitcast(BF16)

        mlp_in_done = sem("mlp_in_done")
        mixes_in = sem("mixes_in")
        gates_in = sem("gates_in")
        bias_in = sem("bias_in")
        x_in = [[sem(f"x_in{i}_{n}") for n in range(NB)] for i in range(2)]
        w_in = [sem(f"w_in{i}") for i in range(NB * NG)]
        w_signed = sem("w_signed")
        constants = sem("constants")
        cut_steps = sem("cut_steps")
        stacked = sem("stacked")
        gate_ready = sem("gate_ready")
        warmed = sem("warmed")
        hidden = sem("hidden")
        gelu_done = sem("gelu_done")
        att_steps = sem("att_steps")
        att_exp = sem("att_exp")
        att_spread = sem("att_spread")
        att_kept = sem("att_kept")
        mix_steps = sem("mix_steps")
        mixed_ready = sem("mixed_ready")
        bias_mm = sem("bias_mm")
        bias_y_ready = sem("bias_y_ready")
        y_mm = sem("y_mm")
        y_ready = sem("y_ready")
        gates_mm = sem("gates_mm")
        gate_parts_ready = sem("gate_parts_ready")
        logits_mm = sem("logits_mm")
        route_steps = sem("route_steps")
        route_exp = sem("route_exp")
        parts_ready = sem("parts_ready")
        route_mm = sem("route_mm")
        route_ready = sem("route_ready")
        scale_mm = sem("scale_mm")
        z_ready = sem("z_ready")
        z_hi = sem("z_hi")
        z_lo = sem("z_lo")
        out_scale_mm = sem("out_scale_mm")
        out_scale_ready = sem("out_scale_ready")
        main_mm = sem("main_mm")
        scaled = sem("scaled")
        result_ready = sem("result_ready")
        x_biased = sem("x_biased")
        stored = [sem(f"stored{i}") for i in range(2)]

        block = ctx.enter_context(nc.Block())

        CONSTANTS = 6 + 2 + GC

        def chunk(c):
            return slice(c * P, (c + 1) * P)

        def columns(n):
            return slice(n * NW, (n + 1) * NW)

        def group(g):
            return slice(g * GC, (g + 1) * GC)

        def by_chunk(b):
            return b[:, :].rearrange("p (c t) -> p c t", c=GC)

        def steps(engine, step):
            for b in range(2):
                step(b, 0, b, True, True)
            with nc.Fori(1, B // 2 - 1, engines=(engine.engine,), hint_back_edge=True) as pair:
                for odd in range(2):
                    step(2 * pair + odd, pair, odd, True, False)
            for b in (B - 2, B - 1):
                step(b, B // 2 - 1, b % 2, b + 1 < B, False)

        w_pieces = ffn_wT.rearrange("(g c p) (n w) -> n g p c w", p=P, c=GC, w=NW)

        @block.sync
        def _(sp):
            sp.dma_start(mlp_in[:, :], mlp).then_inc(mlp_in_done, DMA)
            sp.dma_start(gate_scales_in[:, :], gate_scales).then_inc(gates_in, DMA)
            sp.dma_start(mix_w[:, :, :], mixT).then_inc(mixes_in, DMA)
            for u in range(NB * NG):
                if u >= W_AHEAD:
                    sp.wait_ge(w_in[u - W_AHEAD], DMA)
                n, g = u // NG, u % NG
                sp.dma_start(w_loaded[:, n, group(g), :], w_pieces[n, g]).then_inc(w_in[u], DMA)
                if u == 0:
                    for n in range(NB):
                        sp.dma_start(xs[0][:, columns(n)], x[0, :, columns(n)]).then_inc(x_in[0][n], DMA)
                if u == W_AHEAD - 1:
                    sp.wait_ge(cut_steps, 5)
                    for j in range(PARTS):
                        for i in range(PARTS):
                            row = (PARTS * j + i) * E
                            sp.dma_start(stack[row:row + E, :, :, :].rearrange("e h s f -> e h (s f)"),
                                         cuts[:, j, :, :].rearrange("p s f -> p (s f)")).then_inc(stacked, DMA)
                if u == NG:
                    for n in range(NB):
                        sp.dma_start(xs[1][:, columns(n)], x[1, :, columns(n)]).then_inc(x_in[1][n], DMA)
                if u == NG + 2:
                    sp.dma_start(bias_rows[:, :], ffn_bias.partition_broadcast(P)).then_inc(bias_in, DMA)

            def step(b, pair, odd, more, early):
                for n in range(NB):
                    sp.wait_ge(result_ready, NB * b + n + 1)
                    sp.dma_start(out[bass.ds(b, 1), :, columns(n)].rearrange("o p w -> (o p) w"),
                                 results[n % 2][:, :]).then_inc(stored[n % 2], DMA)
                    if isinstance(b, int) and b + 2 >= B:
                        continue
                    sp.dma_start(xs[odd][:, columns(n)],
                                 x[bass.ds(b + 2, 1), :, columns(n)].rearrange("o p w -> (o p) w"))\
                      .then_inc(x_in[odd][n], DMA)

            steps(sp, step)
            for i in range(2):
                sp.wait_ge(stored[i], DMA * B * NB // 2)

        @block.gpsimd
        def _(pool):
            nc.gpsimd.memset(ones[:, :], 1.0).then_inc(constants, 1)
            nc.gpsimd.memset(unit32[:, :], 0.0).then_inc(constants, 1)
            nc.gpsimd.memset(unit[:, :], 0.0).then_inc(constants, 1)
            nc.gpsimd.memset(fold[:, :], 0.0).then_inc(constants, 1)
            nc.gpsimd.memset(mixed_b[:, :], 0.0).then_inc(constants, 1)
            nc.gpsimd.memset(gate[:, NC * E:], 0.0).then_inc(constants, 1)
            pool.wait_ge(constants, 6)
            for m, n in ((unit32, 32), (unit, P)):
                nc.gpsimd.affine_select(out=m[:, :], in_=m[:, :], compare_op=ALU.not_equal, fill=1.0,
                                        base=0, pattern=[[-1, n]], channel_multiplier=1).then_inc(constants, 1)
            for quarter in range(GC):
                pool.wait_ge(constants, 8 + quarter)
                nc.gpsimd.affine_select(out=fold[:, :], in_=fold[:, :], compare_op=ALU.not_equal, fill=1.0,
                                        base=-quarter * P // GC, pattern=[[-1, E]], channel_multiplier=1)\
                  .then_inc(constants, 1)
            pool.wait_ge(gates_in, DMA)
            nc.gpsimd.tensor_copy(gate[:, 0:NC * E], gate_scales_in[:, 0:P]).then_inc(gate_ready, 1)
            nc.gpsimd.tensor_copy(cuts[:, 0, :, :], cut_in[:, :, :]).then_inc(cut_steps, 1)
            pool.wait_ge(cut_steps, 1)
            nc.gpsimd.tensor_tensor(cut_rest[:, :, :], cut_in[:, :, :], cuts[:, 0, :, :],
                                    ALU.subtract).then_inc(cut_steps, 1)
            pool.wait_ge(cut_steps, 2)
            nc.gpsimd.tensor_copy(cuts[:, 1, :, :], cut_rest[:, :, :]).then_inc(cut_steps, 1)
            pool.wait_ge(cut_steps, 3)
            nc.gpsimd.tensor_tensor(cut_rest[:, :, :], cut_rest[:, :, :], cuts[:, 1, :, :],
                                    ALU.subtract).then_inc(cut_steps, 1)
            pool.wait_ge(cut_steps, 4)
            nc.gpsimd.tensor_copy(cuts[:, 2, :, :], cut_rest[:, :, :]).then_inc(cut_steps, 1)

            def add_bias(q, odd):
                pool.wait_ge(y_mm, NG * q + NG)
                for n in range(NB):
                    nc.gpsimd.tensor_tensor(xs[odd][:, columns(n)], xs[odd][:, columns(n)],
                                            bias_rows[:, columns(n)], ALU.add).then_inc(x_biased, 1)

            pool.wait_ge(bias_in, DMA)
            add_bias(0, 0)

            def step(b, pair, odd, more, early):
                if more:
                    add_bias(b + 1, 1 - odd)

            steps(pool, step)

        @block.scalar
        def _(act):
            signed = [0]

            def sign_pieces(until):
                for u in range(signed[0], until):
                    n, c = u // SPB, u % SPB * SC
                    if c % GC == 0:
                        act.wait_ge(w_in[NG * n + c // GC], DMA)
                    nc.scalar.activation(signs[:, n, c:c + SC, :], w_loaded[:, n, c:c + SC, :],
                                         ACT.Sign).then_inc(w_signed, 1)
                signed[0] = until

            def high(g, q, odd):
                act.wait_ge(z_ready, NG * q + g + 1)
                nc.scalar.activation(halves[odd][:, group(g), 0, :], y[:, group(g), :], ACT.Copy).then_inc(z_hi, 1)

            def keep_bias(q):
                act.wait_ge(bias_mm, q + 1)
                nc.scalar.activation(bias_y[:, :], bias_sum, ACT.Copy).then_inc(bias_y_ready, 1)

            def keep_gate_parts(q):
                act.wait_ge(gates_mm, q + 1)
                nc.scalar.activation(gate_parts[:, :], gate_sum, ACT.Copy).then_inc(gate_parts_ready, 1)

            def route_exps(q):
                act.wait_ge(route_steps, 7 * q + 1)
                nc.scalar.activation(exps[:, :], route_logits, ACT.Exp, bias=top[:, :],
                                     accum_out=total[:, :]).then_inc(route_exp, 1)

            def keep_route(q, odd):
                act.wait_ge(route_mm, q + 1)
                nc.scalar.activation(routeT[odd][:, :], routeT_ps, ACT.Copy).then_inc(route_ready, 1)

            def keep_out_scale(b, n, first=False):
                act.wait_ge(out_scale_mm, NB * b + n + 1)
                if not first:
                    act.wait_ge(scaled, NB * b + n)
                nc.scalar.activation(out_scale[:, :], scale_bank[:, :], ACT.Copy).then_inc(out_scale_ready, 1)

            act.wait_ge(constants, 1)
            nc.scalar.activation(warm[:, :], ones[0:1, 0:1], ACT.Gelu).then_inc(warmed, 1)
            act.wait_ge(mlp_in_done, DMA)
            act.wait_ge(hidden, 1)
            nc.scalar.activation(h1[:, :], ring[0][:, 0:B], ACT.Gelu, bias=b0c).then_inc(gelu_done, 1)
            act.wait_ge(hidden, 2)
            nc.scalar.activation(h2[:, :], ring[1][:, 0:B], ACT.Gelu, bias=b1c).then_inc(gelu_done, 1)
            act.wait_ge(warmed, 1)
            nc.scalar.activation(warm[:, :], ones[0:1, 0:1], ACT.Exp).then_inc(warmed, 1)
            act.wait_ge(att_steps, 2)
            nc.scalar.activation(exps[0:B, :], logits[:, :], ACT.Exp, bias=top[0:B, :],
                                 accum_out=total[0:B, :]).then_inc(att_exp, 1)
            sign_pieces(2)
            keep_bias(0)
            sign_pieces(6)
            keep_gate_parts(0)
            route_exps(0)
            sign_pieces(SPB)
            keep_route(0, 0)
            for g in range(NG):
                high(g, 0, 0)

            def step(b, pair, odd, more, early):
                q, nxt = b + 1, 1 - odd
                loading = early and odd == 0
                keep_out_scale(b, 0, first=loading)
                if more:
                    keep_bias(q)
                if loading:
                    sign_pieces(2 * SPB)
                keep_out_scale(b, 1)
                if more:
                    keep_gate_parts(q)
                if loading:
                    sign_pieces(2 * SPB + 2)
                if more:
                    route_exps(q)
                if loading:
                    sign_pieces(2 * SPB + 3)
                if more:
                    keep_route(q, nxt)
                if loading:
                    sign_pieces(3 * SPB)
                keep_out_scale(b, 2)
                if more:
                    for g in range(NG):
                        if loading:
                            sign_pieces(3 * SPB + 2 * (g + 1))
                        high(g, q, nxt)
                keep_out_scale(b, 3)

            steps(act, step)

        @block.tensor
        def _(pe):
            def bias_product(q):
                pe.wait_ge(mixed_ready, 2 * q + 2)
                nc.tensor.matmul(bias_sum, ones[:, :], mixed_b[:, :], start=True, stop=True).then_inc(bias_mm, 1)

            def y_chunk(q, pair_q, odd, c, first=False):
                if c == 0:
                    pe.wait_ge(mixed_ready, 2 * q + 2)
                g = c // GC
                if c % GC == 0:
                    pe.wait_ge(x_in[odd][g], DMA * (pair_q + 1))
                if c % GC == 0 and not first:
                    pe.wait_ge(z_ready, NG * q - NG + g + 1)
                done = nc.tensor.matmul(ring[g][:, chunk(c % GC)], xs[odd][:, chunk(c)], mixed[:, :],
                                        start=True, stop=True)
                if c % GC == GC - 1:
                    done.then_inc(y_mm, 1)

            def gate_chunks(q):
                pe.wait_ge(bias_y_ready, q + 1)
                for c in range(NC):
                    if c % GC == 0:
                        pe.wait_ge(y_ready, NG * q + c // GC + 1)
                    quarter = slice(c % GC * P // GC, (c % GC + 1) * P // GC)
                    done = nc.tensor.matmul(gate_sum[quarter, :], gate[:, E * c:E * c + P // GC], y[:, c, :],
                                            start=(c < GC), stop=(c >= NC - GC))
                done.then_inc(gates_mm, 1)

            def gate_fold(q):
                pe.wait_ge(gate_parts_ready, q + 1)
                nc.tensor.matmul(route_logits, gate_parts[:, :], fold[:, :], start=True, stop=True)\
                  .then_inc(logits_mm, 1)

            def route_transpose(q):
                pe.wait_ge(parts_ready, q + 1)
                nc.tensor.transpose(routeT_ps, parts[:, :, :, :].rearrange("p j i e -> p (j i e)"),
                                    unit[:, :]).then_inc(route_mm, 1)

            def in_scale_chunk(q, odd, c):
                g = c // GC
                if c == 0:
                    pe.wait_ge(route_ready, q + 1)
                if c % GC == 0:
                    pe.wait_ge(y_ready, NG * q + g + 1)
                done = nc.tensor.matmul(ring[g][:, chunk(c % GC)], stack[:, c, 0, :], routeT[odd][:, :],
                                        start=True, stop=True)
                if c % GC == GC - 1:
                    done.then_inc(scale_mm, 1)

            def out_scale_block(b, odd, n, first=False):
                if not first:
                    pe.wait_ge(out_scale_ready, NB * b + n)
                nc.tensor.matmul(by_chunk(scale_bank), routeT[odd][:, :], stack[:, group(n), 1, :],
                                 start=True, stop=True).then_inc(out_scale_mm, 1)

            pe.wait_ge(mlp_in_done, DMA)
            nc.tensor.matmul(ring[0][:, 0:B], w0, emb, start=True, stop=True).then_inc(hidden, 1)
            pe.wait_ge(gelu_done, 1)
            nc.tensor.matmul(ring[1][:, 0:B], w1, h1[:, :], start=True, stop=True).then_inc(hidden, 1)
            pe.wait_ge(gelu_done, 2)
            nc.tensor.matmul(ring[2][0:B, 0:E], h2[:, :], w2, start=True, stop=True).then_inc(hidden, 1)
            pe.wait_ge(constants, CONSTANTS)
            pe.wait_ge(att_steps, 5)
            nc.tensor.matmul(ring[3][:, 0:B * E], ones[0:B, :], att_wide[:, :, :].rearrange("b c e -> b (c e)"),
                             start=True, stop=True).then_inc(att_spread, 1)
            nc.tensor.matmul(ring[2][0:E, E:E + B], att[:, :], unit32[:, :], start=True, stop=True)\
              .then_inc(att_spread, 1)
            with pe.Fori(0, WARM_UP // 8):
                for _ in range(8):
                    nc.tensor.matmul(main[0][:, 0:P], unit[:, :], unit[:, :], start=True, stop=True)
            bias_product(0)
            for c in range(NC):
                y_chunk(0, 0, 0, c, first=True)
            pe.wait_ge(gate_ready, 1)
            gate_chunks(0)
            gate_fold(0)
            route_transpose(0)
            pe.wait_ge(stacked, DMA * PARTS * PARTS)
            for c in range(NC):
                in_scale_chunk(0, 0, c)

            def step(b, pair, odd, more, early):
                q, nxt = b + 1, 1 - odd
                loading = early and odd == 0
                for m in range(NB * MM):
                    n, k, half = m // MM, m % MM // 2, m % 2
                    if m % MM == 0:
                        out_scale_block(b, odd, n, first=loading and n == 0)
                        if not (loading and n < 2):
                            pe.wait_ge(scaled, NB * b + n - 1)
                    if loading and half == 0 and k % SC == 0:
                        pe.wait_ge(w_signed, n * SPB + k // SC + 1)
                    if n == 0 and half == 0 and k % GC == 0:
                        pe.wait_ge(z_hi, NG * b + k // GC + 1)
                        pe.wait_ge(z_lo, NG * b + k // GC + 1)
                    done = nc.tensor.matmul(main[n % 2][:, :], halves[odd][:, k, half, :],
                                            signs[:, n, k, :],
                                            start=(m % MM == 0), stop=(m % MM == MM - 1))
                    if m % MM == MM - 1:
                        done.then_inc(main_mm, 1)
                    if not more:
                        continue
                    if m == BIAS_AT:
                        bias_product(q)
                    if m in range(Y_AT, Y_AT + 2 * NC, 2):
                        y_chunk(q, pair + odd, nxt, (m - Y_AT) // 2)
                    if m == GATE_AT:
                        gate_chunks(q)
                    if m == FOLD_AT:
                        gate_fold(q)
                    if m == ROUTE_AT:
                        route_transpose(q)
                    if m == SCALE_AT:
                        for c in range(NC):
                            in_scale_chunk(q, nxt, c)

            steps(pe, step)

        @block.vector
        def _(dve):
            def mix(q):
                nc.vector.tensor_copy(att_q[:, :], att_rows[:, bass.ds(q, 1), :].rearrange("p o e -> p (o e)"))\
                  .then_inc(mix_steps, 1)
                nc.vector.tensor_scalar(mixed_b[0:E, :], mix_b, attT[:, bass.ds(q, 1)], None,
                                        ALU.mult).then_inc(mix_steps, 1)
                base = 2 * E * q + 2
                for k in range(E):
                    for right in range(2):
                        half = slice(right * P // 2, (right + 1) * P // 2)
                        if k == 0:
                            if not right:
                                dve.wait_ge(mix_steps, base)
                            done = nc.vector.tensor_scalar(mixed[:, half], mix_w[:, 0, half], att_q[:, 0:1], None,
                                                           ALU.mult)
                        else:
                            dve.wait_ge(mix_steps, base + 2 * k - 1 + right)
                            done = nc.vector.scalar_tensor_tensor(mixed[:, half], mix_w[:, k, half],
                                                                  att_q[:, k:k + 1], mixed[:, half],
                                                                  ALU.mult, ALU.add)
                        done.then_inc(mix_steps if k < E - 1 else mixed_ready, 1)

            def y_sum(q, g):
                dve.wait_ge(y_mm, NG * q + g + 1)
                if g == 0:
                    dve.wait_ge(bias_y_ready, q + 1)
                nc.vector.tensor_tensor(y[:, group(g), :], by_chunk(ring[g]),
                                        bias_y[:, :].unsqueeze(1).to_broadcast([P, GC, T]),
                                        ALU.add).then_inc(y_ready, 1)

            def low(q, odd, g):
                dve.wait_ge(z_hi, NG * q + g + 1)
                nc.vector.tensor_tensor(halves[odd][:, group(g), 1, :], y[:, group(g), :],
                                        halves[odd][:, group(g), 0, :].bitcast(F32), ALU.subtract).then_inc(z_lo, 1)

            def z_product(q, g):
                dve.wait_ge(scale_mm, NG * q + g + 1)
                nc.vector.tensor_tensor(y[:, group(g), :], y[:, group(g), :], by_chunk(ring[g]),
                                        ALU.mult).then_inc(z_ready, 1)

            def routing(q):
                dve.wait_ge(logits_mm, q + 1)
                nc.vector.tensor_reduce(top[:, :], route_logits, AX_X, ALU.max, negate=True)\
                  .then_inc(route_steps, 1)
                dve.wait_ge(route_exp, q + 1)
                nc.vector.reciprocal(inverse[:, :], total[:, :]).then_inc(route_steps, 1)
                dve.wait_ge(route_steps, 7 * q + 2)
                nc.vector.tensor_scalar(route[:, :], exps[:, :], inverse[:, :], None, ALU.mult)\
                  .then_inc(route_steps, 1)
                of = route[:, :]
                for i in range(PARTS):
                    dve.wait_ge(route_steps, 7 * q + 3 + 2 * i)
                    done = nc.vector.tensor_copy(parts[:, :, i, :], of.unsqueeze(1).to_broadcast([P, PARTS, E]))
                    if i == PARTS - 1:
                        done.then_inc(parts_ready, 1)
                        break
                    done.then_inc(route_steps, 1)
                    dve.wait_ge(route_steps, 7 * q + 4 + 2 * i)
                    nc.vector.tensor_tensor(rest[:, i, :], of, parts[:, 0, i, :], ALU.subtract)\
                      .then_inc(route_steps, 1)
                    of = rest[:, i, :]

            def finish(b, odd, n, first=False):
                dve.wait_ge(main_mm, NB * b + n + 1)
                dve.wait_ge(out_scale_ready, NB * b + n + 1)
                if not first:
                    dve.wait_ge(stored[n % 2], DMA * (NB // 2 * b + n // 2))
                nc.vector.tensor_tensor(results[n % 2][:, :], main[n % 2][:, :], out_scale[:, :],
                                        ALU.mult).then_inc(scaled, 1)
                dve.wait_ge(x_biased, NB * b + n + 1)
                dve.wait_ge(scaled, NB * b + n + 1)
                nc.vector.tensor_tensor(results[n % 2][:, :], results[n % 2][:, :], xs[odd][:, columns(n)],
                                        ALU.add).then_inc(result_ready, 1)

            dve.wait_ge(mlp_in_done, DMA)
            dve.wait_ge(hidden, 3)
            nc.vector.tensor_tensor(logits[:, :], ring[2][0:B, 0:E], b2r, ALU.add).then_inc(att_steps, 1)
            dve.wait_ge(att_steps, 1)
            nc.vector.tensor_reduce(top[0:B, :], logits[:, :], AX_X, ALU.max, negate=True).then_inc(att_steps, 1)
            dve.wait_ge(att_exp, 1)
            nc.vector.reciprocal(inverse[0:B, :], total[0:B, :]).then_inc(att_steps, 1)
            dve.wait_ge(att_steps, 3)
            nc.vector.tensor_scalar(att[:, :], exps[0:B, :], inverse[0:B, :], None, ALU.mult).then_inc(att_steps, 1)
            dve.wait_ge(att_steps, 4)
            dve.wait_ge(constants, CONSTANTS)
            nc.vector.tensor_tensor(att_wide[:, :, :], att[:, :].unsqueeze(1).to_broadcast([B, B, E]),
                                    unit32[:, :].unsqueeze(2).to_broadcast([B, B, E]), ALU.mult)\
              .then_inc(att_steps, 1)
            dve.wait_ge(att_spread, 2)
            nc.vector.tensor_copy(att_rows[:, :, :].rearrange("p b e -> p (b e)"), ring[3][:, 0:B * E])\
              .then_inc(att_kept, 1)
            nc.vector.tensor_copy(attT[:, :], ring[2][0:E, E:E + B]).then_inc(att_kept, 1)
            dve.wait_ge(att_kept, 2)
            dve.wait_ge(mixes_in, DMA)
            mix(0)

            def z_halves(q, odd):
                z_product(q, 0)
                for g in range(1, NG):
                    z_product(q, g)
                    low(q, odd, g - 1)
                low(q, odd, NG - 1)

            for g in range(NG):
                y_sum(0, g)
            routing(0)
            mix(1)
            z_halves(0, 0)

            def step(b, pair, odd, more, early):
                q, nxt = b + 1, 1 - odd
                last_prepared = isinstance(b, int) and b + 2 >= B
                if not (early and odd == 0):
                    finish(b - 1, nxt, NB - 1)
                if more:
                    for g in range(NG):
                        y_sum(q, g)
                finish(b, odd, 0, first=early and odd == 0)
                if more:
                    routing(q)
                finish(b, odd, 1, first=early and odd == 0)
                if more:
                    if not last_prepared:
                        mix(q + 1)
                    z_halves(q, nxt)
                finish(b, odd, 2)
                if isinstance(b, int) and b == B - 1:
                    finish(b, odd, NB - 1)

            steps(dve, step)


def kernel(**inputs):
    import concourse.bacc as bacc
    from concourse.bass_utils import run_bass_kernel_spmd

    a = {name: np.asarray(v) for name, v in inputs.items()}
    B, T, H = a["x"].shape
    E = a["L0_cond_W2"].shape[1]
    P_ = 128

    def padded(v):
        return np.concatenate([v, np.zeros((P_ - v.shape[0], v.shape[1]), v.dtype)])

    mlp = [a["cond_128"].T, a["L0_cond_W0"], a["L0_cond_W1"], a["L0_cond_W2"], a["L0_cond_b0"][:, None],
           a["L0_cond_b1"][:, None], np.broadcast_to(a["L0_cond_b2"], (B, E)), a["L0_cond_bias_k"]]
    gate_scales = [a["L0_ffn_gate_w"].reshape(E, H // P_, P_).transpose(2, 1, 0).reshape(P_, -1),
                   a["L0_ffn_in_channel_scale"].reshape(P_, -1), a["L0_ffn_out_channel_scale"].reshape(P_, -1)]
    laid = {
        "x": a["x"],
        "mlp": np.concatenate([padded(v) for v in mlp], 1),
        "mixT": a["L0_cond_weight"][..., 0].transpose(2, 0, 1),
        "ffn_wT": a["L0_ffn_weight"].T,
        "ffn_bias": a["L0_ffn_bias"],
        "gate_scales": np.concatenate(gate_scales, 1),
    }
    laid = {name: np.ascontiguousarray(v) for name, v in laid.items()}
    nc = bacc.Bacc("TRN2", target_bir_lowering=False, num_devices=1, dynamic_dma_scratch_size=1024)
    args = {name: nc.dram_tensor(f"in_{name}", v.shape, mybir.dt.from_np(v.dtype), kind="ExternalInput").ap()
            for name, v in laid.items()}
    out = nc.dram_tensor("out_0", (B, T, H), F32, kind="ExternalOutput").ap()
    adaln_ffn(nc, *args.values(), out)
    r = run_bass_kernel_spmd(nc, [{f"in_{name}": v for name, v in laid.items()}], core_ids=[0])
    return r.results[0]["out_0"]
```
